# Optimizing a Trainium2 kernel written in Bass

```python
import numpy as np
import jax
import jax.numpy as jnp

def _softmax(x, axis=-1):
    return jax.nn.softmax(x, axis=axis)

def _gelu(x):
    return jax.nn.gelu(x, approximate=True)

def _silu(x):
    return jax.nn.silu(x)

def _sigmoid(x):
    return jax.nn.sigmoid(x)

def _layernorm(x, axis=-1, eps=1e-05):
    m = jnp.mean(x, axis=axis, keepdims=True)
    v = jnp.var(x, axis=axis, keepdims=True)
    return (x - m) / jnp.sqrt(v + eps)

def _scatter_add(tgt, idx, src, axis=0):
    return tgt.at[idx].add(src)

def _segment_sum(src, seg, n):
    return jax.ops.segment_sum(src, seg, n)
kernel_name = 'mk_adj_resnorm_d2_adj_r2_151f9c'

def setup_inputs(seed: int=0):
    np.random.seed(seed)
    _w = jnp.asarray

    def _rec_inputs():
        import jax
        import jax.numpy as jnp
        _gk = jax.random.key(seed)
        x = -0.003407 + 1.001 * jax.random.normal(jax.random.fold_in(_gk, 1), (64, 128, 128), jnp.float32)
        _a = jax.random.bernoulli(jax.random.fold_in(_gk, 2), 0.125, (64, 128, 128))
        _a = jnp.logical_or(_a, jnp.swapaxes(_a, -1, -2))
        _a = jnp.logical_or(_a, jnp.eye(128, dtype=bool))
        _af = _a.astype(jnp.float32)
        _af = _af * jax.random.uniform(jax.random.fold_in(_gk, 3), (64, 128, 128), jnp.float32, 0.05, 1)
        adj = _af
        return (x, adj)
    x, adj = _rec_inputs()

    def _L0_gnn_setup():
        import jax, jax.numpy as jnp
        import numpy as np
        B, S, H, HID = (1, 512, 128, 128)
        LN_EPS = 1e-05

        def _layernorm(y, gamma, beta):
            mu = jnp.mean(y, axis=-1, keepdims=True)
            var = jnp.mean(jnp.square(y - mu), axis=-1, keepdims=True)
            return (y - mu) * jax.lax.rsqrt(var + LN_EPS) * gamma + beta
        key = jax.random.key(seed)
        ks = jax.random.split(key, 8)
        x = jax.random.normal(ks[0], (B, S, H), dtype=jnp.float32)
        adj = jax.random.uniform(ks[1], (B, S, S), dtype=jnp.float32)
        W1 = jax.random.normal(ks[2], (2 * H, HID), dtype=jnp.float32) / np.sqrt(2 * H)
        b1 = jnp.zeros((HID,), dtype=jnp.float32)
        W2 = jax.random.normal(ks[3], (HID, HID), dtype=jnp.float32) / np.sqrt(HID)
        b2 = jnp.zeros((HID,), dtype=jnp.float32)
        gamma = jnp.ones((HID,), dtype=jnp.float32)
        beta = jnp.zeros((HID,), dtype=jnp.float32)
        return {'x': x, 'adj': adj, 'W1': W1, 'b1': b1, 'W2': W2, 'b2': b2, 'gamma': gamma, 'beta': beta}
    _L0_gnn_all = _L0_gnn_setup()
    _L0_gnn_in = {k: v for k, v in _L0_gnn_all.items() if k in ('W1', 'b1', 'W2', 'b2', 'gamma', 'beta')}
    del _L0_gnn_all

    def _L1_gnn_setup():
        import jax, jax.numpy as jnp
        import numpy as np
        C = 128
        key = jax.random.key(seed)
        k_h, k_A, k_Ww, k_Wb, k_aw, k_ab = jax.random.split(key, 6)
        B, N = (8, 1024)
        h = jax.random.normal(k_h, (B, N, C), dtype=jnp.float32)
        A = jax.random.uniform(k_A, (B, N, N), dtype=jnp.float32)
        lim_W = 1.0 / np.sqrt(C)
        W_w = jax.random.uniform(k_Ww, (C, C), minval=-lim_W, maxval=lim_W, dtype=jnp.float32)
        W_b = jax.random.uniform(k_Wb, (C,), minval=-lim_W, maxval=lim_W, dtype=jnp.float32)
        lim_a = 1.0 / np.sqrt(2 * C)
        a_w = jax.random.uniform(k_aw, (2 * C,), minval=-lim_a, maxval=lim_a, dtype=jnp.float32)
        a_b = jax.random.uniform(k_ab, (), minval=-lim_a, maxval=lim_a, dtype=jnp.float32)
        return {'h': h, 'A': A, 'W_w': W_w, 'W_b': W_b, 'a_w': a_w, 'a_b': a_b}
    _L1_gnn_all = _L1_gnn_setup()
    _L1_gnn_in = {k: v for k, v in _L1_gnn_all.items() if k in ('W_w', 'W_b', 'a_w', 'a_b')}
    del _L1_gnn_all
    return {'x': x, 'adj': adj, 'L0_gnn_W1': _L0_gnn_in['W1'], 'L0_gnn_b1': _L0_gnn_in['b1'], 'L0_gnn_W2': _L0_gnn_in['W2'], 'L0_gnn_b2': _L0_gnn_in['b2'], 'L0_gnn_gamma': _L0_gnn_in['gamma'], 'L0_gnn_beta': _L0_gnn_in['beta'], 'L1_gnn_W_w': _L1_gnn_in['W_w'], 'L1_gnn_W_b': _L1_gnn_in['W_b'], 'L1_gnn_a_w': _L1_gnn_in['a_w'], 'L1_gnn_a_b': _L1_gnn_in['a_b']}

def reference(x, adj, L0_gnn_W1, L0_gnn_b1, L0_gnn_W2, L0_gnn_b2, L0_gnn_gamma, L0_gnn_beta, L1_gnn_W_w, L1_gnn_W_b, L1_gnn_a_w, L1_gnn_a_b):
    import jax
    import jax.numpy as jnp

    def _L0_gnn_ref(x, adj, W1, b1, W2, b2, gamma, beta):
        import jax, jax.numpy as jnp
        import numpy as np
        B, S, H, HID = (1, 512, 128, 128)
        LN_EPS = 1e-05

        def _layernorm(y, gamma, beta):
            mu = jnp.mean(y, axis=-1, keepdims=True)
            var = jnp.mean(jnp.square(y - mu), axis=-1, keepdims=True)
            return (y - mu) * jax.lax.rsqrt(var + LN_EPS) * gamma + beta
        hi = jnp.einsum('bsh,hk->bsk', x, W1[:H])
        hj = jnp.einsum('bsh,hk->bsk', x, W1[H:])
        h = jax.nn.relu(hi[:, :, None, :] + hj[:, None, :, :] + b1)
        y = jnp.einsum('bijk,kl->bijl', h, W2) + b2
        y = _layernorm(y, gamma, beta)
        out = jnp.einsum('bij,bijh->bih', adj, y)
        return out

    def _L1_gnn_ref(h, A, W_w, W_b, a_w, a_b):
        import jax, jax.numpy as jnp
        import numpy as np
        C = 128
        Wh = jnp.einsum('bnc,dc->bnd', h, W_w) + W_b
        si = Wh @ a_w[:C]
        sj = Wh @ a_w[C:]
        s = si[:, :, None] + sj[:, None, :] + a_b
        e = jnp.exp(s) * A
        alpha = e / jnp.sum(e, axis=2, keepdims=True)
        h_prime = jnp.einsum('bij,bjc->bic', alpha, h)
        return h_prime
    x = _layernorm(x + _L0_gnn_ref(x, adj, L0_gnn_W1, L0_gnn_b1, L0_gnn_W2, L0_gnn_b2, L0_gnn_gamma, L0_gnn_beta), axis=-1)
    x = _layernorm(x + _L1_gnn_ref(x, adj, L1_gnn_W_w, L1_gnn_W_b, L1_gnn_a_w, L1_gnn_a_b), axis=-1)
    return x

_drawn_inputs = setup_inputs


def setup_inputs(seed=0):
    import zlib

    import numpy as np

    out = dict(_drawn_inputs(seed))
    spreads = {'L0_gnn_b1': (0.0, 0.1),
     'L0_gnn_b2': (0.0, 0.1),
     'L0_gnn_gamma': (1.0, 0.2),
     'L0_gnn_beta': (0.0, 0.1)}
    factors = {'L1_gnn_W_w': 3.976, 'L1_gnn_W_b': 8.0, 'L1_gnn_a_w': 3.81}
    for name, (base, spread) in spreads.items():
        noise = np.random.default_rng([zlib.crc32(name.encode()), seed]).standard_normal(out[name].shape)
        drawn = base * np.exp(spread * noise) if base else spread * noise
        out[name] = jnp.asarray(drawn.astype(out[name].dtype))
    for name, factor in factors.items():
        out[name] = (out[name] * factor).astype(out[name].dtype)
    return out
```

```python
from contextlib import ExitStack
from math import sqrt

import concourse.bass as bass
from concourse import mybir


def gnn_pair_kernel(nc, x, adj, W1, b1, W2, b2, gamma, beta, Ww, Wb, aw, ab, out):
    F32 = mybir.dt.float32
    ALU = mybir.AluOpType
    ACT = mybir.ActivationFunctionType

    B, S, H = x.shape
    K = W2.shape[0]
    EPS = 1e-5
    UNIT = 8
    UNITS = S // UNIT
    QUART = 4
    QUARTS = S // QUART
    QPU = UNIT // QUART
    HRING = 4
    YRING = 4
    GROUPS, GROUP = 4, 32
    LAST = S - 1
    PEEL, LOOP_END = 4, B - 2

    AGG_FIRST, AGG_PER_UNIT = 4, 3

    ctx = ExitStack()
    with ctx:
        def sb(name, shape):
            return ctx.enter_context(nc.sbuf_tensor(name, shape, F32))

        def ps(name, shape):
            return ctx.enter_context(nc.psum_tensor(name, shape, F32))

        def sem(name):
            return ctx.enter_context(nc.semaphore(name))

        w1a, w1b = sb("w1a", [H, K]), sb("w1b", [H, K])
        w2, w2T = sb("w2", [K, K]), sb("w2T", [K, K])
        b1c, b2col, gcol = sb("b1c", [K, 1]), sb("b2col", [K, 1]), sb("gcol", [K, 1])
        beta_rows = sb("beta_rows", [S, K])
        ww, wbc = sb("ww", [K, K]), sb("wbc", [K, 1])
        a1c, a2c, abc = sb("a1c", [K, 1]), sb("a2c", [K, 1]), sb("abc", [S, 1])
        ident, ones = sb("ident", [S, S]), sb("ones", [S, S])
        house, centre = sb("house", [K, K]), sb("centre", [K, K])
        basis, basis_half = sb("basis", [K, K]), sb("basis_half", [K, K])
        b2c, b2c_rep = sb("b2c", [K, 1]), sb("b2c_rep", [K, S])
        gdiag = sb("gdiag", [K, K])
        a1rep, a2rep, wbrep, a12 = sb("a1rep", [K, S]), sb("a2rep", [K, S]), sb("wbrep", [K, S]), sb("a12", [K, 1])
        w_pair = sb("w_pair", [K, K])
        w_back = sb("w_back", [K, K])
        v1rep, v2rep = sb("v1rep", [K, S]), sb("v2rep", [K, S])
        score_c = sb("score_c", [S, 1])
        bnorm = sb("bnorm", [S, 1])
        epsc = sb("epsc", [S, 1])

        x_in, adj_in = sb("x_in", [S, 2, H]), sb("adj_in", [S, 2, S])
        x_res = sb("x_res", [S, 2, H])
        xT = sb("xT", [H, S])
        adjT, adjS = sb("adjT", [S, 2, S]), sb("adjS", [S, 2, S])
        aT, bT = sb("aT", [K, 2, S]), sb("bT", [K, 2, S])
        h = sb("h", [K, HRING, UNIT, S])
        y = sb("y", [S, 2, S, K])
        squares = sb("squares", [S, YRING, QUART, K])
        q = sb("q", [S, 2, S])
        v, sd = sb("v", [S, S]), sb("sd", [S, S])
        rstd = sb("rstd", [S, S])
        wz = sb("wz", [S, S, GROUP])
        o_sb, oT_sb = sb("o_sb", [S, K]), sb("oT_sb", [K, S])
        x1p, x1e, x1T = sb("x1p", [S, K]), sb("x1e", [S, K + 1]), sb("x1T", [K, S])
        st1, mv1, sd1, rs1 = sb("st1", [S, 6]), sb("mv1", [S, 2]), sb("sd1", [S, 1]), sb("rs1", [S, 1])
        ex, eT = sb("ex", [S, S]), sb("eT", [S, S])
        rz, x2p = sb("rz", [S, 1]), sb("x2p", [S, K])
        st2, mv2, sd2, rs2 = sb("st2", [S, 6]), sb("mv2", [S, 2]), sb("sd2", [S, 1]), sb("rs2", [S, 1])
        x_out = sb("x_out", [S, 2, K])

        y_ps = [ps(f"y_ps{n}", [S, QUART, K]) for n in range(YRING)]
        agg_ps = ps("agg_ps", [S, 512])
        prep_ps = ps("prep_ps", [S, 4, 128])
        tail_ps = ps("tail_ps", [S, 4, 128])
        att_ps = ps("att_ps", [S, 512])

        s_w = sem("weights_loaded")
        s_const = sem("constants_built")
        s_setup_pe = sem("setup_products")
        s_setup_dve = sem("setup_vector_steps")
        s_ready = sem("setup_done")
        s_zero = sem("buffers_preset")
        x_loaded, adj_loaded, xres_loaded, stored = (
            [sem(f"{n}_{p}") for p in range(2)] for n in ("x_loaded", "adj_loaded", "xres_loaded", "out_stored"))
        xT_ps_s, adjT_ps_s, adjT_sb_s = sem("xT_in_psum"), sem("adjT_in_psum"), sem("adjT_in_sbuf")
        ab_ps_s, ab_sb_s = sem("ab_in_psum"), sem("ab_in_sbuf")
        u_ready, h_ready = sem("preact_ready"), sem("h_ready")
        y_in_psum, y_stored, q_done = sem("y_in_psum"), sem("y_stored"), sem("q_done")
        v_ready, sd_ready, rstd_ready, w_ready = sem("v_ready"), sem("sd_ready"), sem("rstd_ready"), sem("w_ready")
        agg_done, o_stored, oT_ps_s, oT_sb_s, f_ps_s = sem("agg_done"), sem("o_stored"), sem("oT_in_psum"), sem("oT_in_sbuf"), sem("f_in_psum")
        x1p_ready, st1_ready, mv1_ready, sd1_ready, rs1_ready = sem("x1p_ready"), sem("st1_ready"), sem("mv1_ready"), sem("sd1_ready"), sem("rs1_ready")
        x1_ready, x1T_ps_s, x1T_sb_s, score_ps_s = sem("x1_ready"), sem("x1T_in_psum"), sem("x1T_in_sbuf"), sem("scores_in_psum")
        ex_ready, eT_ready, att_done = sem("exp_ready"), sem("eT_ready"), sem("attention_in_psum")
        rz_ready, x2p_ready, st2_ready, mv2_ready, sd2_ready, rs2_ready = sem("rz_ready"), sem("x2p_ready"), sem("st2_ready"), sem("mv2_ready"), sem("sd2_ready"), sem("rs2_ready")
        s_passed = sem("statistics_wait_passed")
        out_ready = sem("out_ready")

        def run_slots(engine, slot):
            for t in range(PEEL):
                slot(t, t // 2, t % 2, True, True, t >= 1, t >= 2, t)
            with engine.Fori(PEEL // 2, LOOP_END // 2) as pair:
                for p in range(2):
                    slot(pair * 2 + p, pair, p, True, True, True, True, PEEL)
            for t in range(LOOP_END, B + 2):
                slot(t, t // 2, t % 2, t < B, t + 1 < B, t <= B, True, PEEL)

        def nth16(half, p, off):
            return (half + (p + off) // 2 + 1) * 16

        block = ctx.enter_context(nc.Block())

        @block.sync
        def _(sp):
            col = lambda a: a.rearrange("(p o) -> p o", o=1)
            sp.dma_start(w2[:], W2[:, :]).then_inc(s_w, 16)
            sp.dma_start(b2col[:], col(b2)).then_inc(s_w, 16)
            sp.dma_start(gcol[:], col(gamma)).then_inc(s_w, 16)
            sp.dma_start(ww[:], Ww[:, :]).then_inc(s_w, 16)
            sp.dma_start(wbc[:], col(Wb)).then_inc(s_w, 16)
            sp.dma_start(a1c[:], col(aw[0:K])).then_inc(s_w, 16)
            sp.dma_start(a2c[:], col(aw[K:2 * K])).then_inc(s_w, 16)
            sp.dma_start(abc[:], ab.broadcast_to([S, 1])).then_inc(s_w, 16)
            sp.dma_start(w1a[:], W1[0:H, :]).then_inc(s_w, 16)
            sp.dma_start(w1b[:], W1[H:2 * H, :]).then_inc(s_w, 16)
            sp.dma_start(b1c[:], col(b1)).then_inc(s_w, 16)
            sp.dma_start(beta_rows[:], beta.rearrange("(o k) -> o k", o=1).broadcast_to([S, K])).then_inc(s_w, 16)
            for b in range(2):
                sp.dma_start(x_in[:, b, :], x[b]).then_inc(x_loaded[b], 16)
                sp.dma_start(adj_in[:, b, :], adj[b]).then_inc(adj_loaded[b], 16)

            def slot(t, half, p, pairs, prep, gather, tail, early):
                if pairs and not (isinstance(t, int) and t + 2 >= B):
                    sp.wait_ge(xT_ps_s, t + 1)
                    sp.dma_start(x_in[:, p, :], x[bass.ds(t + 2, 1)].rearrange("o s h -> (o s) h")).then_inc(x_loaded[p], 16)
                    sp.wait_ge(adjT_ps_s, t + 1)
                    sp.dma_start(adj_in[:, p, :], adj[bass.ds(t + 2, 1)].rearrange("o s h -> (o s) h")).then_inc(adj_loaded[p], 16)
                if gather:
                    if early >= 3:
                        sp.wait_ge(x1p_ready, t - 2)
                    sp.dma_start(x_res[:, 1 - p, :], x[bass.ds(t - 1, 1)].rearrange("o s h -> (o s) h")).then_inc(xres_loaded[1 - p], 16)
                if tail:
                    sp.wait_ge(out_ready, t - 1)
                    sp.dma_start(out[bass.ds(t - 2, 1)].rearrange("o s h -> (o s) h"), x_out[:, p, :]).then_inc(stored[p], 16)

            run_slots(sp, slot)
            for p in range(2):
                sp.wait_ge(stored[p], 16 * (B // 2))

        @block.gpsimd
        def _(pool):
            nc.gpsimd.memset(ident[:], 0.0).then_inc(s_const, 1)
            nc.gpsimd.memset(house[:], -1.0 / (K - sqrt(K))).then_inc(s_const, 1)
            nc.gpsimd.memset(ones[:], 1.0).then_inc(s_const, 1)
            pool.wait_ge(s_const, 3)
            nc.gpsimd.affine_select(out=ident[:], in_=ident[:], compare_op=ALU.not_equal, fill=1.0, base=0,
                                    pattern=[[-1, S]], channel_multiplier=1).then_inc(s_const, 1)
            nc.gpsimd.affine_select(out=house[:], in_=house[:], compare_op=ALU.not_equal, fill=1.0 / sqrt(K),
                                    base=-(K - 1), pattern=[[0, K]], channel_multiplier=1).then_inc(s_const, 1)
            nc.gpsimd.memset(epsc[:], EPS).then_inc(s_const, 1)
            nc.gpsimd.memset(wz[:], 0.0).then_inc(s_zero, 1)

            def slot(t, half, p, pairs, prep, gather, tail, early):
                if not pairs:
                    return
                for u in range(UNITS):
                    if u == 0:
                        pool.wait_ge(ab_sb_s, t + 1)
                    if not (early == 0 and u < HRING):
                        pool.wait_ge(y_in_psum, t * QUARTS + (u - HRING + 1) * QPU)
                    nc.gpsimd.tensor_tensor(
                        h[:, u % HRING],
                        bT[:, p, :].unsqueeze(1).broadcast_to([K, UNIT, S]),
                        aT[:, p, u * UNIT:(u + 1) * UNIT].unsqueeze(2).broadcast_to([K, UNIT, S]),
                        ALU.add).then_inc(u_ready, 1)

            run_slots(pool, slot)

        @block.scalar
        def _(act):
            def copy(dst, src):
                return nc.scalar.activation(dst, src, ACT.Copy)

            def prep_copies(b, early):
                act.wait_ge(adjT_ps_s, b + 1)
                if early >= 1:
                    act.wait_ge(ab_ps_s, b)
                copy(xT[:], prep_ps[:, 0, :])
                if early >= 2:
                    act.wait_ge(w_ready, b - 1)

            def relu(t, u):
                act.wait_ge(u_ready, t * UNITS + u + 1)
                nc.scalar.activation(h[:, u % HRING], h[:, u % HRING], ACT.Relu).then_inc(h_ready, 1)

            prep_copies(0, 0)
            copy(adjT[:, 0, :], prep_ps[:, 1, :]).then_inc(adjT_sb_s, 1)
            for u in range(2):
                relu(0, u)

            def slot(t, half, p, pairs, prep, gather, tail, early):
                for u in range(UNITS):
                    if tail and u == 0:
                        act.wait_ge(agg_done, t - 1)
                        if early >= 3:
                            act.wait_ge(oT_ps_s, t - 2)
                        copy(o_sb[:], agg_ps[:, 0:K]).then_inc(o_stored, 1)
                    if gather and u == 2:
                        act.wait_ge(v_ready, t)
                        if early >= 2:
                            act.wait_ge(rstd_ready, t - 1)
                        nc.scalar.activation(sd[:], v[:], ACT.Sqrt, bias=epsc[:, 0:1], scale=1.0 / K).then_inc(sd_ready, 1)
                    if tail and u == 2:
                        act.wait_ge(oT_ps_s, t - 1)
                        if early >= 3:
                            act.wait_ge(f_ps_s, t - 2)
                        copy(oT_sb[:], tail_ps[:, 0, :]).then_inc(oT_sb_s, 1)
                    if tail and u == 5:
                        act.wait_ge(mv1_ready, t - 1)
                        if early >= 3:
                            act.wait_ge(rs1_ready, t - 2)
                        nc.scalar.activation(sd1[:], mv1[:, 1:2], ACT.Sqrt, bias=epsc[:, 0:1]).then_inc(sd1_ready, 1)
                    if prep and u == 6:
                        prep_copies(t + 1, early + 1)
                        copy(adjT[:, 1 - p, :], prep_ps[:, 1, :]).then_inc(adjT_sb_s, 1)
                    if tail and u == 8:
                        act.wait_ge(x1T_ps_s, t - 1)
                        if early >= 3:
                            act.wait_ge(score_ps_s, t - 2)
                        copy(x1T[:], tail_ps[:, 2, :]).then_inc(x1T_sb_s, 1)
                    if tail and u == 10:
                        act.wait_ge(score_ps_s, t - 1)
                        if early >= 3:
                            act.wait_ge(eT_ready, t - 2)
                        nc.scalar.activation(ex[:], tail_ps[:, 3, :], ACT.Exp, bias=score_c[:, 0:1]).then_inc(ex_ready, 1)
                    if tail and u == 14:
                        act.wait_ge(mv2_ready, t - 1)
                        if early >= 3:
                            act.wait_ge(rs2_ready, t - 2)
                        nc.scalar.activation(sd2[:], mv2[:, 1:2], ACT.Sqrt, bias=epsc[:, 0:1]).then_inc(sd2_ready, 1)
                    if pairs:
                        ahead = u + 2
                        if ahead < UNITS:
                            relu(t, ahead)
                        elif prep:
                            relu(t + 1, ahead - UNITS)
                        for k in range(u * QPU, (u + 1) * QPU):
                            if k == 0 and early >= 2:
                                act.wait_ge(agg_done, t - 1)
                            if k == 0 and early == 0:
                                act.wait_ge(s_zero, 3)
                            act.wait_ge(y_in_psum, t * QUARTS + k + 1)
                            copy(y[:, p, k * QUART:(k + 1) * QUART, 0:LAST],
                                 y_ps[k % YRING][:, :, 0:LAST]).then_inc(y_stored, 1)

            run_slots(act, slot)

        @block.vector
        def _(dve):
            for p in range(2):
                nc.vector.memset(y[:, p, :, LAST:S], 2.0).then_inc(s_zero, 1)
            nc.vector.memset(x1e[:], 1.0).then_inc(s_setup_dve, 1)
            dve.wait_ge(s_const, 6)
            dve.wait_ge(s_w, 16 * 12)
            nc.vector.tensor_scalar(centre[:], ident[:], -1.0 / K, None, ALU.add).then_inc(s_setup_dve, 1)
            nc.vector.tensor_tensor(basis[:], house[:], ident[:], ALU.add).then_inc(s_setup_dve, 1)
            nc.vector.tensor_scalar(gdiag[:], ident[:], gcol[:, 0:1], None, ALU.mult).then_inc(s_setup_dve, 1)
            nc.vector.tensor_scalar(a1rep[:], ones[:], a1c[:, 0:1], None, ALU.mult).then_inc(s_setup_dve, 1)
            nc.vector.tensor_scalar(a2rep[:], ones[:], a2c[:, 0:1], None, ALU.mult).then_inc(s_setup_dve, 1)
            nc.vector.tensor_scalar(wbrep[:], ones[:], wbc[:, 0:1], None, ALU.mult).then_inc(s_setup_dve, 1)
            nc.vector.tensor_tensor(a12[:], a1c[:], a2c[:], ALU.add).then_inc(s_setup_dve, 1)
            dve.wait_ge(s_setup_pe, 5)
            dve.wait_ge(s_setup_dve, 8)
            nc.vector.tensor_copy(b2c[:], att_ps[:, 0:1]).then_inc(s_setup_dve, 1)
            nc.vector.tensor_copy(basis[:, LAST:S], att_ps[:, 0:1]).then_inc(s_setup_dve, 1)
            dve.wait_ge(s_setup_dve, 10)
            nc.vector.tensor_scalar(b2c_rep[:], ones[:], b2c[:, 0:1], None, ALU.mult).then_inc(s_setup_dve, 1)
            nc.vector.tensor_copy(basis_half[:, 0:LAST], basis[:, 0:LAST]).then_inc(s_setup_dve, 1)
            nc.vector.tensor_scalar(basis_half[:, LAST:S], basis[:, LAST:S], 0.5, None, ALU.mult).then_inc(s_setup_dve, 1)
            nc.vector.tensor_copy(w2T[:], tail_ps[:, 0, :]).then_inc(s_setup_dve, 1)
            nc.vector.tensor_copy(v1rep[:], tail_ps[:, 1, :]).then_inc(s_ready, 1)
            nc.vector.tensor_copy(v2rep[:], tail_ps[:, 2, :]).then_inc(s_ready, 1)
            nc.vector.tensor_tensor(score_c[:], tail_ps[:, 3, 0:1], abc[:], ALU.add).then_inc(s_ready, 1)
            dve.wait_ge(s_setup_pe, 8)
            nc.vector.tensor_copy(bnorm[:], att_ps[:, 1:2]).then_inc(s_ready, 1)
            nc.vector.tensor_copy(w_pair[:], agg_ps[:, 0:K]).then_inc(s_ready, 1)
            nc.vector.tensor_copy(w_back[:], agg_ps[:, K:2 * K]).then_inc(s_ready, 1)
            dve.wait_ge(s_ready, 6)

            def project(b, p):
                dve.wait_ge(ab_ps_s, b + 1)
                nc.vector.tensor_copy(aT[:, p, :], prep_ps[:, 2, :])
                nc.vector.tensor_scalar(bT[:, p, :], prep_ps[:, 3, :], b1c[:, 0:1], None, ALU.add).then_inc(ab_sb_s, 1)

            project(0, 0)

            def slot(t, half, p, pairs, prep, gather, tail, early):
                for u in range(UNITS):
                    if gather and u == 0:
                        dve.wait_ge(q_done, t * QUARTS)
                        if early >= 2:
                            dve.wait_ge(sd_ready, t - 1)
                        nc.vector.tensor_scalar(v[:], q[:, 1 - p, :], bnorm[:, 0:1], 0.0, ALU.add, ALU.max).then_inc(v_ready, 1)
                    if gather and u == 2:
                        dve.wait_ge(sd_ready, t)
                        nc.vector.reciprocal(rstd[:], sd[:]).then_inc(rstd_ready, 1)
                        dve.wait_ge(adjT_sb_s, t)
                        nc.vector.tensor_copy(adjS[:, 1 - p, :], adjT[:, 1 - p, :])
                        dve.wait_ge(rstd_ready, t)
                        if early >= 2:
                            dve.wait_ge(agg_done, t - 1)
                        else:
                            dve.wait_ge(s_zero, 3)
                        diag = wz[:].rearrange("j (g r) c -> j g (r c)", g=GROUPS)[:, :, 0:GROUP * GROUP:GROUP + 1]
                        nc.vector.tensor_tensor(diag, adjT[:, 1 - p, :].rearrange("j (g r) -> j g r", g=GROUPS),
                                                rstd[:].rearrange("j (g r) -> j g r", g=GROUPS), ALU.mult).then_inc(w_ready, 1)
                    if tail and u == 3:
                        dve.wait_ge(f_ps_s, t - 1)
                        dve.wait_ge(xres_loaded[p], nth16(half, p, -2))
                        nc.vector.tensor_tensor(x1p[:], tail_ps[:, 1, :], x_res[:, p, :], ALU.add).then_inc(x1p_ready, 1)
                        dve.wait_ge(x1p_ready, t - 1)
                        nc.vector.bn_stats(st1[:], x1p[:]).then_inc(st1_ready, 1)
                        dve.wait_ge(st1_ready, t - 1)
                        dve.sem_inc(s_passed, 1)
                        nc.vector.bn_aggr(mv1[:], st1[:]).then_inc(mv1_ready, 1)
                    if tail and u == 5:
                        dve.wait_ge(sd1_ready, t - 1)
                        nc.vector.reciprocal(rs1[:], sd1[:]).then_inc(rs1_ready, 1)
                        dve.wait_ge(rs1_ready, t - 1)
                        nc.vector.tensor_scalar(x1e[:, 0:K], x1p[:], mv1[:, 0:1], rs1[:, 0:1], ALU.subtract, ALU.mult).then_inc(x1_ready, 1)
                    if prep and u == 8:
                        if early >= 1:
                            dve.wait_ge(u_ready, t * UNITS)
                        project(t + 1, 1 - p)
                    if tail and u == 10:
                        dve.wait_ge(ex_ready, t - 1)
                        nc.vector.tensor_tensor(eT[:], ex[:], adjS[:, p, :], ALU.mult).then_inc(eT_ready, 1)
                    if tail and u == 12:
                        dve.wait_ge(att_done, t - 1)
                        nc.vector.reciprocal(rz[:], att_ps[:, K:K + 1]).then_inc(rz_ready, 1)
                        dve.wait_ge(rz_ready, t - 1)
                        nc.vector.scalar_tensor_tensor(out=x2p[:], in0=att_ps[:, 0:K], scalar=rz[:, 0:1], in1=x1e[:, 0:K],
                                                       op0=ALU.mult, op1=ALU.add).then_inc(x2p_ready, 1)
                        dve.wait_ge(x2p_ready, t - 1)
                        nc.vector.bn_stats(st2[:], x2p[:]).then_inc(st2_ready, 1)
                        dve.wait_ge(st2_ready, t - 1)
                        dve.sem_inc(s_passed, 1)
                        nc.vector.bn_aggr(mv2[:], st2[:]).then_inc(mv2_ready, 1)
                    if tail and u == 14:
                        dve.wait_ge(sd2_ready, t - 1)
                        nc.vector.reciprocal(rs2[:], sd2[:]).then_inc(rs2_ready, 1)
                        dve.wait_ge(rs2_ready, t - 1)
                        if early >= 4:
                            dve.wait_ge(stored[p], nth16(half, p, -4))
                        nc.vector.tensor_scalar(x_out[:, p, :], x2p[:], mv2[:, 0:1], rs2[:, 0:1], ALU.subtract, ALU.mult).then_inc(out_ready, 1)
                    if pairs:
                        for k in range(u * QPU, (u + 1) * QPU):
                            dve.wait_ge(y_stored, t * QUARTS + k + 1)
                            for n in range(QUART):
                                i = k * QUART + n
                                last = nc.vector.tensor_tensor_reduce(
                                    out=squares[:, k % YRING, n, :], in0=y_ps[k % YRING][:, n, :], in1=y[:, p, i, :], scale=1.0, scalar=0.0,
                                    op0=ALU.mult, op1=ALU.add, accum_out=q[:, p, i:i + 1])
                            last.then_inc(q_done, 1)

            run_slots(dve, slot)

        @block.tensor
        def _(pe):
            def mm(dst, lhsT, rhs, start=True, stop=True):
                return nc.tensor.matmul(dst, lhsT, rhs, start=start, stop=stop)

            pe.wait_ge(s_w, 16 * 12)
            pe.wait_ge(s_const, 6)
            pe.wait_ge(s_setup_dve, 8)
            mm(att_ps[:, 0:1], centre[:], b2col[:]).then_inc(s_setup_pe, 1)
            nc.tensor.transpose(tail_ps[:, 0, :], w2[:], ident[:]).then_inc(s_setup_pe, 1)
            mm(tail_ps[:, 1, :], ww[:], a1rep[:]).then_inc(s_setup_pe, 1)
            mm(tail_ps[:, 2, :], ww[:], a2rep[:]).then_inc(s_setup_pe, 1)
            mm(tail_ps[:, 3, 0:1], wbrep[:], a12[:]).then_inc(s_setup_pe, 1)
            pe.wait_ge(s_setup_dve, 14)
            mm(att_ps[:, 1:2], b2c_rep[:], b2c[:]).then_inc(s_setup_pe, 1)
            mm(agg_ps[:, 0:K], w2T[:], basis[:]).then_inc(s_setup_pe, 1)
            mm(agg_ps[:, K:2 * K], basis_half[:], gdiag[:]).then_inc(s_setup_pe, 1)

            def prep_transposes(b, p, loads, later):
                pe.wait_ge(x_loaded[p], loads)
                if later:
                    pe.wait_ge(ab_sb_s, b)
                nc.tensor.transpose(prep_ps[:, 0, :], x_in[:, p, :], ident[:]).then_inc(xT_ps_s, 1)
                pe.wait_ge(adj_loaded[p], loads)
                nc.tensor.transpose(prep_ps[:, 1, :], adj_in[:, p, :], ident[:]).then_inc(adjT_ps_s, 1)

            def prep_products(b):
                pe.wait_ge(adjT_sb_s, b + 1)
                mm(prep_ps[:, 2, :], w1a[:], xT[:])
                mm(prep_ps[:, 3, :], w1b[:], xT[:]).then_inc(ab_ps_s, 1)

            prep_transposes(0, 0, 16, False)
            prep_products(0)
            pe.wait_ge(s_ready, 6)

            def slot(t, half, p, pairs, prep, gather, tail, early):
                quad = 0
                for u in range(UNITS):
                    if tail and u == 1:
                        pe.wait_ge(o_stored, t - 1)
                        nc.tensor.transpose(tail_ps[:, 0, :], o_sb[:], ident[:]).then_inc(oT_ps_s, 1)
                    if tail and u == 3:
                        pe.wait_ge(oT_sb_s, t - 1)
                        mm(tail_ps[:, 1, :], oT_sb[:], w_back[:], True, False)
                        mm(tail_ps[:, 1, :], adjS[:, p, :], beta_rows[:], False, True).then_inc(f_ps_s, 1)
                    if prep and u == 5:
                        prep_transposes(t + 1, 1 - p, nth16(half, p, 1), True)
                    if prep and u == 7:
                        prep_products(t + 1)
                    if tail and u == 7:
                        pe.wait_ge(x1_ready, t - 1)
                        nc.tensor.transpose(tail_ps[:, 2, :], x1e[:, 0:K], ident[:]).then_inc(x1T_ps_s, 1)
                    if tail and u == 9:
                        pe.wait_ge(x1T_sb_s, t - 1)
                        mm(tail_ps[:, 3, :], v1rep[:], x1T[:], True, False)
                        mm(tail_ps[:, 3, :], x1T[:], v2rep[:], False, True).then_inc(score_ps_s, 1)
                    if tail and u == 12:
                        pe.wait_ge(eT_ready, t - 1)
                        mm(att_ps[:, 0:K + 1], eT[:], x1e[:]).then_inc(att_done, 1)
                    if pairs:
                        pe.wait_ge(h_ready, t * UNITS + u + 1)
                        for k in range(u * QPU, (u + 1) * QPU):
                            if not (early == 0 and k < YRING):
                                pe.wait_ge(q_done, t * QUARTS + k - YRING + 1)
                            for n in range(QUART):
                                last = mm(y_ps[k % YRING][:, n, :], h[:, u % HRING, (k % QPU) * QUART + n, :], w_pair[:])
                            last.then_inc(y_in_psum, 1)
                    if gather and u >= AGG_FIRST:
                        if u == AGG_FIRST:
                            pe.wait_ge(w_ready, t)
                            if early >= 2:
                                pe.wait_ge(o_stored, t - 1)
                        for r in range(quad, min(quad + AGG_PER_UNIT, GROUP)):
                            for g in range(GROUPS):
                                i = g * GROUP + r
                                last = nc.tensor.matmul(agg_ps[g * GROUP:(g + 1) * GROUP, 0:K], wz[:, i, :], y[:, 1 - p, i, :],
                                                        start=(r == 0), stop=(r == GROUP - 1), tile_position=(0, g * GROUP))
                            if r == GROUP - 1:
                                last.then_inc(agg_done, 1)
                        quad = min(quad + AGG_PER_UNIT, GROUP)

            run_slots(pe, slot)


_INS = ["x", "adj", "L0_gnn_W1", "L0_gnn_b1", "L0_gnn_W2", "L0_gnn_b2", "L0_gnn_gamma", "L0_gnn_beta",
        "L1_gnn_W_w", "L1_gnn_W_b", "L1_gnn_a_w", "L1_gnn_a_b"]


def kernel(**inputs):
    import numpy as _np
    import concourse.bacc as _bacc
    from concourse import mybir as _mybir
    from concourse.bass_utils import run_bass_kernel_spmd as _run

    nc = _bacc.Bacc("TRN2", target_bir_lowering=False, num_devices=1)
    arrays, args = {}, []
    for name in _INS:
        a = _np.ascontiguousarray(inputs[name])
        if a.ndim == 0:
            a = a.reshape(1, 1)
        arrays[f"in_{name}_dram"] = a
        args.append(nc.dram_tensor(f"in_{name}_dram", a.shape, _mybir.dt.from_np(a.dtype), kind="ExternalInput").ap())
    out = nc.dram_tensor("out_dram", inputs["x"].shape, _mybir.dt.float32, kind="ExternalOutput").ap()
    gnn_pair_kernel(nc, *args, out)
    r = _run(nc, [arrays], core_ids=[0])
    return r.results[0]["out_dram"]
```

```python
from contextlib import ExitStack
from math import sqrt

import concourse.bass as bass
from concourse import mybir


def gnn_pair_kernel(nc, x, adj, W1, b1, W2, b2, gamma, beta, Ww, Wb, aw, ab, out):
    F32 = mybir.dt.float32
    ALU = mybir.AluOpType
    ACT = mybir.ActivationFunctionType

    B, S, H = x.shape
    K = W2.shape[0]
    EPS = 1e-5
    UNIT = 8
    UNITS = S // UNIT
    QUART = 4
    QUARTS = S // QUART
    QPU = UNIT // QUART
    HRING = 4
    YRING = 4
    GROUPS, GROUP = 4, 32
    LAST = S - 1
    PEEL, LOOP_END = 4, B - 2

    CHUNK = 4
    CHUNKS = GROUP // CHUNK
    WEIGHTS_UNIT = 4
    CHUNK_STEP = UNITS // CHUNKS
    EARLY_CHUNKS = (UNITS - WEIGHTS_UNIT) // CHUNK_STEP

    ctx = ExitStack()
    with ctx:
        def sb(name, shape):
            return ctx.enter_context(nc.sbuf_tensor(name, shape, F32))

        def ps(name, shape):
            return ctx.enter_context(nc.psum_tensor(name, shape, F32))

        def sem(name):
            return ctx.enter_context(nc.semaphore(name))

        w1a, w1b = sb("w1a", [H, K]), sb("w1b", [H, K])
        w2, w2T = sb("w2", [K, K]), sb("w2T", [K, K])
        b1c, b2col, gcol = sb("b1c", [K, 1]), sb("b2col", [K, 1]), sb("gcol", [K, 1])
        beta_rows = sb("beta_rows", [S, K])
        ww, wbc = sb("ww", [K, K]), sb("wbc", [K, 1])
        a1c, a2c, abc = sb("a1c", [K, 1]), sb("a2c", [K, 1]), sb("abc", [S, 1])
        ident, ones = sb("ident", [S, S]), sb("ones", [S, S])
        house, centre = sb("house", [K, K]), sb("centre", [K, K])
        basis, basis_half = sb("basis", [K, K]), sb("basis_half", [K, K])
        b2c, b2c_rep = sb("b2c", [K, 1]), sb("b2c_rep", [K, S])
        gdiag = sb("gdiag", [K, K])
        a1rep, a2rep, wbrep, a12 = sb("a1rep", [K, S]), sb("a2rep", [K, S]), sb("wbrep", [K, S]), sb("a12", [K, 1])
        w_pair = sb("w_pair", [K, K])
        w_back = sb("w_back", [K, K])
        v1row, v2row = sb("v1row", [S, K]), sb("v2row", [S, K])
        score_c = sb("score_c", [S, 1])
        bnorm = sb("bnorm", [S, 1])
        epsc = sb("epsc", [S, 1])

        x_in, adj_in = sb("x_in", [S, 2, H]), sb("adj_in", [S, 2, S])
        x_res, adj_res = sb("x_res", [S, 2, H]), sb("adj_res", [S, 2, S])
        adj_sum, x_beta = sb("adj_sum", [S, 1]), sb("x_beta", [S, H])
        sj, si, si_cols, s_terms = sb("sj", [S, 1]), sb("si", [S, 1]), sb("si_cols", [S, S]), sb("s_terms", [S, 2, K])
        xT = sb("xT", [H, S])
        adjT, adjS = sb("adjT", [S, 2, S]), sb("adjS", [S, 2, S])
        aT, bT = sb("aT", [K, 2, S]), sb("bT", [K, 2, S])
        h = sb("h", [K, HRING, UNIT, S])
        y = sb("y", [S, 2, S, K])
        squares = ctx.enter_context(nc.sbuf_tensor("squares", [S, YRING, QUART, K], mybir.dt.bfloat16))
        q = sb("q", [S, 2, S])
        v, sd = sb("v", [S, S]), sb("sd", [S, S])
        rstd = sb("rstd", [S, S])
        wz = sb("wz", [S, S, GROUP])
        o_sb, oT_sb = sb("o_sb", [S, K]), sb("oT_sb", [K, S])
        x1p, x1e = sb("x1p", [S, K]), sb("x1e", [S, K + 1])
        st1, mv1, sd1, rs1 = sb("st1", [S, 6]), sb("mv1", [S, 2]), sb("sd1", [S, 1]), sb("rs1", [S, 1])
        ex, eT = sb("ex", [S, S]), sb("eT", [S, S])
        rz, x2p = sb("rz", [S, 1]), sb("x2p", [S, K])
        st2, mv2, sd2, rs2 = sb("st2", [S, 6]), sb("mv2", [S, 2]), sb("sd2", [S, 1]), sb("rs2", [S, 1])
        x_out = sb("x_out", [S, K])

        y_ps = [ps(f"y_ps{n}", [S, QUART, K]) for n in range(YRING)]
        agg_ps = ps("agg_ps", [S, 512])
        prep_ps = ps("prep_ps", [S, 4, 128])
        tail_ps = ps("tail_ps", [S, 4, 128])
        att_ps = ps("att_ps", [S, 512])

        s_w, s_w1 = sem("weights_loaded"), sem("first_layer_weights_loaded")
        s_const = sem("constants_built")
        s_setup_pe = sem("setup_products")
        s_setup_dve = sem("setup_vector_steps")
        s_ready = sem("setup_done")
        s_two, s_zero = sem("twos_preset"), sem("wz_zeroed")
        x_loaded, adj_loaded, xres_loaded, stored = (
            [sem(f"{n}_{p}") for p in range(2)] for n in ("x_loaded", "adj_loaded", "xres_loaded", "out_stored"))
        xT_ps_s, adjT_ps_s, adjT_sb_s = sem("xT_in_psum"), sem("adjT_in_psum"), sem("adjT_in_sbuf")
        ab_ps_s, ab_sb_s = sem("ab_in_psum"), sem("ab_in_sbuf")
        u_ready, h_ready = sem("preact_ready"), sem("h_ready")
        y_in_psum, y_stored, q_done = sem("y_in_psum"), sem("y_stored"), sem("q_done")
        v_ready, sd_ready, rstd_ready, w_ready = sem("v_ready"), sem("sd_ready"), sem("rstd_ready"), sem("w_ready")
        agg_done, o_stored, oT_ps_s, oT_sb_s, f_ps_s = sem("agg_done"), sem("o_stored"), sem("oT_in_psum"), sem("oT_in_sbuf"), sem("f_in_psum")
        x1p_ready, st1_ready, mv1_ready, sd1_ready, rs1_ready = sem("x1p_ready"), sem("st1_ready"), sem("mv1_ready"), sem("sd1_ready"), sem("rs1_ready")
        x1_ready, score_ps_s = sem("x1_ready"), sem("scores_in_psum")
        ex_ready, eT_ready, att_done = sem("exp_ready"), sem("eT_ready"), sem("attention_in_psum")
        rz_ready, x2p_ready, st2_ready, mv2_ready, sd2_ready, rs2_ready = sem("rz_ready"), sem("x2p_ready"), sem("st2_ready"), sem("mv2_ready"), sem("sd2_ready"), sem("rs2_ready")
        adj_sum_ready, x_beta_ready, sj_ready, si_sum_ready, si_ready = (
            sem(n) for n in ("adj_sum_ready", "x_beta_ready", "sj_ready", "si_sum_ready", "si_ready"))
        s_passed = sem("statistics_wait_passed")
        out_ready = sem("out_ready")

        def run_slots(engine, slot):
            for t in range(PEEL):
                slot(t, t // 2, t % 2, True, True, t >= 1, t >= 2, t >= 3, t)
            with engine.Fori(PEEL // 2, LOOP_END // 2) as pair:
                for p in range(2):
                    slot(pair * 2 + p, pair, p, True, True, True, True, True, PEEL)
            for t in range(LOOP_END, B + 3):
                slot(t, t // 2, t % 2, t < B, t + 1 < B, t <= B, t <= B + 1, True, PEEL)

        def nth16(half, p, off):
            return (half + (p + off) // 2 + 1) * 16

        block = ctx.enter_context(nc.Block())

        @block.sync
        def _(sp):
            for b in range(2):
                sp.dma_start(x_in[:, b, :], x[b]).then_inc(x_loaded[b], 16)
                sp.dma_start(adj_in[:, b, :], adj[b]).then_inc(adj_loaded[b], 16)
                if b == 0:
                    sp.dma_start(w1a[:], W1[0:H, :]).then_inc(s_w1, 16)
                    sp.dma_start(w1b[:], W1[H:2 * H, :]).then_inc(s_w1, 16)
                    sp.dma_start(b1c[:], b1.rearrange("(p o) -> p o", o=1)).then_inc(s_w1, 16)

            def slot(t, half, p, pairs, prep, gather, tail, finish, early):
                if pairs and not (isinstance(t, int) and t + 2 >= B):
                    sp.wait_ge(xT_ps_s, t + 1)
                    sp.dma_start(x_in[:, p, :], x[bass.ds(t + 2, 1)].rearrange("o s h -> (o s) h")).then_inc(x_loaded[p], 16)
                    sp.wait_ge(adjT_ps_s, t + 1)
                    sp.dma_start(adj_in[:, p, :], adj[bass.ds(t + 2, 1)].rearrange("o s h -> (o s) h")).then_inc(adj_loaded[p], 16)
                if gather:
                    if early >= 3:
                        sp.wait_ge(x1p_ready, t - 2)
                    sp.dma_start(x_res[:, 1 - p, :], x[bass.ds(t - 1, 1)].rearrange("o s h -> (o s) h")).then_inc(xres_loaded[1 - p], 16)
                    sp.dma_start(adj_res[:, 1 - p, :], adj[bass.ds(t - 1, 1)].rearrange("o s h -> (o s) h")).then_inc(xres_loaded[1 - p], 16)
                if finish:
                    sp.wait_ge(out_ready, t - 2)
                    sp.dma_start(out[bass.ds(t - 3, 1)].rearrange("o s h -> (o s) h"), x_out[:]).then_inc(stored[1 - p], 16)

            run_slots(sp, slot)
            for p in range(2):
                sp.wait_ge(stored[p], 16 * (B // 2))

        @block.gpsimd
        def _(pool):
            nc.gpsimd.memset(ident[:], 0.0).then_inc(s_const, 1)
            nc.gpsimd.memset(house[:], -1.0 / (K - sqrt(K))).then_inc(s_const, 1)
            nc.gpsimd.memset(ones[:], 1.0).then_inc(s_const, 1)
            pool.wait_ge(s_const, 3)
            nc.gpsimd.affine_select(out=ident[:], in_=ident[:], compare_op=ALU.not_equal, fill=1.0, base=0,
                                    pattern=[[-1, S]], channel_multiplier=1).then_inc(s_const, 1)
            nc.gpsimd.affine_select(out=house[:], in_=house[:], compare_op=ALU.not_equal, fill=1.0 / sqrt(K),
                                    base=-(K - 1), pattern=[[0, K]], channel_multiplier=1).then_inc(s_const, 1)
            nc.gpsimd.memset(epsc[:], EPS).then_inc(s_const, 1)

            def slot(t, half, p, pairs, prep, gather, tail, finish, early):
                if not pairs:
                    return
                for u in range(UNITS):
                    if early == 0 and u == HRING:
                        nc.gpsimd.memset(wz[:], 0.0).then_inc(s_zero, 1)
                    if u == 0:
                        pool.wait_ge(ab_sb_s, t + 1)
                    if not (early == 0 and u < HRING):
                        pool.wait_ge(y_in_psum, t * QUARTS + (u - HRING + 1) * QPU)
                    shape = [K, QPU, GROUPS, S]
                    a_now = aT[:, p, :].rearrange("k (g r) -> k r g", g=GROUPS)[:, u * QPU:(u + 1) * QPU, :]
                    nc.gpsimd.tensor_tensor(
                        h[:, u % HRING].rearrange("k (r g) s -> k r g s", g=GROUPS),
                        bT[:, p, :].unsqueeze(1).unsqueeze(1).broadcast_to(shape),
                        a_now.unsqueeze(3).broadcast_to(shape), ALU.add).then_inc(u_ready, 1)

            run_slots(pool, slot)

        @block.scalar
        def _(act):
            def copy(dst, src):
                return nc.scalar.activation(dst, src, ACT.Copy)

            def prep_copies(b, early):
                act.wait_ge(adjT_ps_s, b + 1)
                if early >= 1:
                    act.wait_ge(ab_ps_s, b)
                copy(xT[:], prep_ps[:, 0, :])
                if early >= 2:
                    act.wait_ge(w_ready, b - 1)

            def relu(t, u):
                act.wait_ge(u_ready, t * UNITS + u + 1)
                nc.scalar.activation(h[:, u % HRING], h[:, u % HRING], ACT.Relu).then_inc(h_ready, 1)

            col = lambda a: a.rearrange("(p o) -> p o", o=1)
            act.dma_start(b2col[:], col(b2)).then_inc(s_w, 16)
            act.dma_start(w2[:], W2[:, :]).then_inc(s_w, 16)
            act.dma_start(gcol[:], col(gamma)).then_inc(s_w, 16)
            act.dma_start(ww[:], Ww[:, :]).then_inc(s_w, 16)
            act.dma_start(wbc[:], col(Wb)).then_inc(s_w, 16)
            act.dma_start(a1c[:], col(aw[0:K])).then_inc(s_w, 16)
            act.dma_start(a2c[:], col(aw[K:2 * K])).then_inc(s_w, 16)
            act.dma_start(abc[:], ab.broadcast_to([S, 1])).then_inc(s_w, 16)
            act.dma_start(beta_rows[:], beta.rearrange("(o k) -> o k", o=1).broadcast_to([S, K])).then_inc(s_w, 16)
            prep_copies(0, 0)
            copy(adjT[:, 0, :], prep_ps[:, 1, :]).then_inc(adjT_sb_s, 1)
            for u in range(2):
                relu(0, u)

            def slot(t, half, p, pairs, prep, gather, tail, finish, early):
                for u in range(UNITS):
                    if gather and u == 2:
                        act.wait_ge(v_ready, t)
                        if early >= 2:
                            act.wait_ge(rstd_ready, t - 1)
                        nc.scalar.activation(sd[:], v[:], ACT.Sqrt, bias=epsc[:, 0:1], scale=1.0 / K).then_inc(sd_ready, 1)
                    if finish and u == 2:
                        act.wait_ge(mv2_ready, t - 2)
                        if early >= 4:
                            act.wait_ge(rs2_ready, t - 3)
                        nc.scalar.activation(sd2[:], mv2[:, 1:2], ACT.Sqrt, bias=epsc[:, 0:1]).then_inc(sd2_ready, 1)
                    if tail and u == 4:
                        act.wait_ge(agg_done, (t - 1) * CHUNKS)
                        if early >= 3:
                            act.wait_ge(oT_ps_s, t - 2)
                        copy(o_sb[:], agg_ps[:, 0:K]).then_inc(o_stored, 1)
                    if tail and u == 6:
                        act.wait_ge(oT_ps_s, t - 1)
                        if early >= 3:
                            act.wait_ge(f_ps_s, t - 2)
                        copy(oT_sb[:], tail_ps[:, 0, :]).then_inc(oT_sb_s, 1)
                    if prep and u == 7:
                        prep_copies(t + 1, early + 1)
                        copy(adjT[:, 1 - p, :], prep_ps[:, 1, :]).then_inc(adjT_sb_s, 1)
                    if tail and u == 9:
                        act.wait_ge(mv1_ready, t - 1)
                        if early >= 3:
                            act.wait_ge(rs1_ready, t - 2)
                        nc.scalar.activation(sd1[:], mv1[:, 1:2], ACT.Sqrt, bias=epsc[:, 0:1]).then_inc(sd1_ready, 1)
                    if tail and u == 14:
                        act.wait_ge(score_ps_s, t - 1)
                        if early >= 3:
                            act.wait_ge(eT_ready, t - 2)
                        act.wait_ge(sj_ready, t - 1)
                        nc.scalar.activation(ex[:], tail_ps[:, 3, :], ACT.Exp, bias=sj[:, 0:1]).then_inc(ex_ready, 1)
                    if pairs:
                        ahead = u + 2
                        if ahead < UNITS:
                            relu(t, ahead)
                        elif prep:
                            relu(t + 1, ahead - UNITS)
                        for k in range(u * QPU, (u + 1) * QPU):
                            if k == 0 and early >= 2:
                                act.wait_ge(agg_done, (t - 2) * CHUNKS + EARLY_CHUNKS)
                            if k == EARLY_CHUNKS * CHUNK and early >= 2:
                                act.wait_ge(agg_done, (t - 1) * CHUNKS)
                            if k == 0 and early == 0:
                                act.wait_ge(s_two, 2)
                            act.wait_ge(y_in_psum, t * QUARTS + k + 1)
                            copy(y[:, p, k * QUART:(k + 1) * QUART, 0:LAST],
                                 y_ps[k % YRING][:, :, 0:LAST]).then_inc(y_stored, 1)

            run_slots(act, slot)

        @block.vector
        def _(dve):
            def project(b, p):
                dve.wait_ge(ab_ps_s, b + 1)
                nc.vector.tensor_copy(aT[:, p, :], prep_ps[:, 2, :])
                nc.vector.tensor_scalar(bT[:, p, :], prep_ps[:, 3, :], b1c[:, 0:1], None, ALU.add).then_inc(ab_sb_s, 1)

            for p in range(2):
                nc.vector.memset(y[:, p, :, LAST:S], 2.0).then_inc(s_two, 1)
            nc.vector.memset(x1e[:], 1.0).then_inc(s_setup_dve, 1)
            dve.wait_ge(s_const, 6)
            nc.vector.tensor_scalar(centre[:], ident[:], -1.0 / K, None, ALU.add).then_inc(s_setup_dve, 1)
            nc.vector.tensor_tensor(basis[:], house[:], ident[:], ALU.add).then_inc(s_setup_dve, 1)
            dve.wait_ge(s_w, 16 * 9)
            nc.vector.tensor_scalar(gdiag[:], ident[:], gcol[:, 0:1], None, ALU.mult).then_inc(s_setup_dve, 1)
            nc.vector.tensor_scalar(a1rep[:], ones[:], a1c[:, 0:1], None, ALU.mult).then_inc(s_setup_dve, 1)
            nc.vector.tensor_scalar(a2rep[:], ones[:], a2c[:, 0:1], None, ALU.mult).then_inc(s_setup_dve, 1)
            nc.vector.tensor_scalar(wbrep[:], ones[:], wbc[:, 0:1], None, ALU.mult).then_inc(s_setup_dve, 1)
            nc.vector.tensor_tensor(a12[:], a1c[:], a2c[:], ALU.add).then_inc(s_setup_dve, 1)
            dve.wait_ge(s_setup_pe, 5)
            dve.wait_ge(s_setup_dve, 8)
            nc.vector.tensor_copy(b2c[:], att_ps[:, 0:1]).then_inc(s_setup_dve, 1)
            nc.vector.tensor_copy(basis[:, LAST:S], att_ps[:, 0:1]).then_inc(s_setup_dve, 1)
            dve.wait_ge(s_setup_dve, 10)
            nc.vector.tensor_scalar(b2c_rep[:], ones[:], b2c[:, 0:1], None, ALU.mult).then_inc(s_setup_dve, 1)
            nc.vector.tensor_copy(basis_half[:, 0:LAST], basis[:, 0:LAST]).then_inc(s_setup_dve, 1)
            nc.vector.tensor_scalar(basis_half[:, LAST:S], basis[:, LAST:S], 0.5, None, ALU.mult).then_inc(s_setup_dve, 1)
            nc.vector.tensor_copy(w2T[:], tail_ps[:, 0, :]).then_inc(s_setup_dve, 1)
            dve.wait_ge(s_w1, 16 * 3)
            project(0, 0)
            nc.vector.tensor_copy(v1row[:], tail_ps[:, 1, :]).then_inc(s_ready, 1)
            nc.vector.tensor_copy(v2row[:], tail_ps[:, 2, :]).then_inc(s_ready, 1)
            nc.vector.tensor_tensor(score_c[:], tail_ps[:, 3, 0:1], abc[:], ALU.add).then_inc(s_ready, 1)
            dve.wait_ge(s_setup_pe, 8)
            nc.vector.tensor_copy(bnorm[:], att_ps[:, 1:2]).then_inc(s_ready, 1)
            nc.vector.tensor_copy(w_pair[:], agg_ps[:, 0:K]).then_inc(s_ready, 1)
            nc.vector.tensor_copy(w_back[:], agg_ps[:, K:2 * K]).then_inc(s_ready, 1)
            dve.wait_ge(s_ready, 6)

            def slot(t, half, p, pairs, prep, gather, tail, finish, early):
                for u in range(UNITS):
                    if gather and u == 0:
                        dve.wait_ge(q_done, t * QUARTS)
                        if early >= 2:
                            dve.wait_ge(sd_ready, t - 1)
                        nc.vector.tensor_scalar(v[:], q[:, 1 - p, :], bnorm[:, 0:1], 0.0, ALU.add, ALU.max).then_inc(v_ready, 1)
                    if finish and u == 0:
                        dve.wait_ge(att_done, t - 2)
                        nc.vector.reciprocal(rz[:], att_ps[:, K:K + 1]).then_inc(rz_ready, 1)
                        dve.wait_ge(rz_ready, t - 2)
                        nc.vector.scalar_tensor_tensor(out=x2p[:], in0=att_ps[:, 0:K], scalar=rz[:, 0:1], in1=x1e[:, 0:K],
                                                       op0=ALU.mult, op1=ALU.add).then_inc(x2p_ready, 1)
                        dve.wait_ge(x2p_ready, t - 2)
                        nc.vector.bn_stats(st2[:], x2p[:]).then_inc(st2_ready, 1)
                        dve.wait_ge(st2_ready, t - 2)
                        dve.sem_inc(s_passed, 1)
                        nc.vector.bn_aggr(mv2[:], st2[:]).then_inc(mv2_ready, 1)
                    if gather and u == 2:
                        dve.wait_ge(sd_ready, t)
                        nc.vector.reciprocal(rstd[:], sd[:]).then_inc(rstd_ready, 1)
                    if finish and u == 2:
                        dve.wait_ge(sd2_ready, t - 2)
                        nc.vector.reciprocal(rs2[:], sd2[:]).then_inc(rs2_ready, 1)
                        dve.wait_ge(rs2_ready, t - 2)
                        if early >= 4:
                            dve.wait_ge(stored[p], nth16(half, p, -4))
                        nc.vector.tensor_scalar(x_out[:], x2p[:], mv2[:, 0:1], rs2[:, 0:1], ALU.subtract, ALU.mult).then_inc(out_ready, 1)
                    if gather and u == 4:
                        dve.wait_ge(adjT_sb_s, t)
                        nc.vector.tensor_copy(adjS[:, 1 - p, :], adjT[:, 1 - p, :])
                        dve.wait_ge(rstd_ready, t)
                        if early >= 2:
                            dve.wait_ge(agg_done, (t - 1) * CHUNKS)
                        else:
                            dve.wait_ge(s_zero, 1)
                        diag = wz[:].rearrange("j (g r) c -> j g (r c)", g=GROUPS)[:, :, 0:GROUP * GROUP:GROUP + 1]
                        nc.vector.tensor_tensor(diag, adjT[:, 1 - p, :].rearrange("j (g r) -> j g r", g=GROUPS),
                                                rstd[:].rearrange("j (r g) -> j g r", g=GROUPS), ALU.mult).then_inc(w_ready, 1)
                    if tail and u == 7:
                        dve.wait_ge(xres_loaded[p], nth16(half, p, -2) * 2)
                        nc.vector.reduce_sum(adj_sum[:], adj_res[:, p, :], axis=mybir.AxisListType.X).then_inc(adj_sum_ready, 1)
                        dve.wait_ge(adj_sum_ready, t - 1)
                        nc.vector.scalar_tensor_tensor(out=x_beta[:], in0=beta_rows[:], scalar=adj_sum[:, 0:1], in1=x_res[:, p, :],
                                                       op0=ALU.mult, op1=ALU.add).then_inc(x_beta_ready, 1)
                        dve.wait_ge(x_beta_ready, t - 1)
                        dve.wait_ge(f_ps_s, t - 1)
                        nc.vector.tensor_tensor(x1p[:], tail_ps[:, 1, :], x_beta[:], ALU.add).then_inc(x1p_ready, 1)
                        dve.wait_ge(x1p_ready, t - 1)
                        nc.vector.bn_stats(st1[:], x1p[:]).then_inc(st1_ready, 1)
                        dve.wait_ge(st1_ready, t - 1)
                        dve.sem_inc(s_passed, 1)
                        nc.vector.bn_aggr(mv1[:], st1[:]).then_inc(mv1_ready, 1)
                    if tail and u == 9:
                        dve.wait_ge(sd1_ready, t - 1)
                        nc.vector.reciprocal(rs1[:], sd1[:]).then_inc(rs1_ready, 1)
                        dve.wait_ge(rs1_ready, t - 1)
                        nc.vector.tensor_scalar(x1e[:, 0:K], x1p[:], mv1[:, 0:1], rs1[:, 0:1], ALU.subtract, ALU.mult).then_inc(x1_ready, 1)
                        dve.wait_ge(x1_ready, t - 1)
                        if early >= 3:
                            dve.wait_ge(ex_ready, t - 2)
                        nc.vector.tensor_tensor_reduce(out=s_terms[:, 0, :], in0=x1e[:, 0:K], in1=v2row[:], scale=1.0, scalar=score_c[:, 0:1],
                                                       op0=ALU.mult, op1=ALU.add, accum_out=sj[:, 0:1]).then_inc(sj_ready, 1)
                        nc.vector.tensor_tensor_reduce(out=s_terms[:, 1, :], in0=x1e[:, 0:K], in1=v1row[:], scale=1.0, scalar=0.0,
                                                       op0=ALU.mult, op1=ALU.add, accum_out=si[:, 0:1]).then_inc(si_sum_ready, 1)
                        dve.wait_ge(si_sum_ready, t - 1)
                        nc.vector.tensor_scalar(si_cols[:], ones[:], si[:, 0:1], None, ALU.mult).then_inc(si_ready, 1)
                    if prep and u == 10:
                        if early >= 1:
                            dve.wait_ge(u_ready, t * UNITS)
                        project(t + 1, 1 - p)
                    if tail and u == 14:
                        dve.wait_ge(ex_ready, t - 1)
                        nc.vector.tensor_tensor(eT[:], ex[:], adjS[:, p, :], ALU.mult).then_inc(eT_ready, 1)
                    if pairs:
                        for k in range(u * QPU, (u + 1) * QPU):
                            dve.wait_ge(y_stored, t * QUARTS + k + 1)
                            for n in range(QUART):
                                i = k * QUART + n
                                last = nc.vector.tensor_tensor_reduce(
                                    out=squares[:, k % YRING, n, :], in0=y_ps[k % YRING][:, n, :], in1=y[:, p, i, :],
                                    scale=1.0, scalar=0.0, op0=ALU.mult, op1=ALU.add, accum_out=q[:, p, i:i + 1])
                            last.then_inc(q_done, 1)

            run_slots(dve, slot)

        @block.tensor
        def _(pe):
            def mm(dst, lhsT, rhs, start=True, stop=True):
                return nc.tensor.matmul(dst, lhsT, rhs, start=start, stop=stop)

            def prep_transposes(b, p, loads, later):
                pe.wait_ge(x_loaded[p], loads)
                if later:
                    pe.wait_ge(ab_sb_s, b)
                nc.tensor.transpose(prep_ps[:, 0, :], x_in[:, p, :], ident[:]).then_inc(xT_ps_s, 1)
                pe.wait_ge(adj_loaded[p], loads)
                nc.tensor.transpose(prep_ps[:, 1, :], adj_in[:, p, :], ident[:]).then_inc(adjT_ps_s, 1)

            def prep_products(b):
                pe.wait_ge(adjT_sb_s, b + 1)
                mm(prep_ps[:, 2, :], w1a[:], xT[:])
                mm(prep_ps[:, 3, :], w1b[:], xT[:]).then_inc(ab_ps_s, 1)

            pe.wait_ge(s_const, 6)
            prep_transposes(0, 0, 16, False)
            pe.wait_ge(s_w, 16 * 9)
            pe.wait_ge(s_setup_dve, 8)
            mm(att_ps[:, 0:1], centre[:], b2col[:]).then_inc(s_setup_pe, 1)
            nc.tensor.transpose(tail_ps[:, 0, :], w2[:], ident[:]).then_inc(s_setup_pe, 1)
            mm(tail_ps[:, 1, :], a1rep[:], ww[:]).then_inc(s_setup_pe, 1)
            mm(tail_ps[:, 2, :], a2rep[:], ww[:]).then_inc(s_setup_pe, 1)
            mm(tail_ps[:, 3, 0:1], wbrep[:], a12[:]).then_inc(s_setup_pe, 1)
            pe.wait_ge(s_w1, 16 * 3)
            prep_products(0)
            pe.wait_ge(s_setup_dve, 14)
            mm(att_ps[:, 1:2], b2c_rep[:], b2c[:]).then_inc(s_setup_pe, 1)
            mm(agg_ps[:, 0:K], w2T[:], basis[:]).then_inc(s_setup_pe, 1)
            mm(agg_ps[:, K:2 * K], basis_half[:], gdiag[:]).then_inc(s_setup_pe, 1)

            pe.wait_ge(s_ready, 6)

            def weighted_sums(b_parity, chunk):
                for r in range(chunk * CHUNK, (chunk + 1) * CHUNK):
                    for g in range(GROUPS):
                        last = nc.tensor.matmul(agg_ps[g * GROUP:(g + 1) * GROUP, 0:K], wz[:, g * GROUP + r, :],
                                                y[:, b_parity, r * GROUPS + g, :],
                                                start=(r == 0), stop=(r == GROUP - 1), tile_position=(0, g * GROUP))
                last.then_inc(agg_done, 1)

            def slot(t, half, p, pairs, prep, gather, tail, finish, early):
                for u in range(UNITS):
                    if finish and u == 0:
                        pe.wait_ge(eT_ready, t - 2)
                        mm(att_ps[:, 0:K + 1], eT[:], x1e[:]).then_inc(att_done, 1)
                    if tail and u == 5:
                        pe.wait_ge(o_stored, t - 1)
                        nc.tensor.transpose(tail_ps[:, 0, :], o_sb[:], ident[:]).then_inc(oT_ps_s, 1)
                    if prep and u == 6:
                        prep_transposes(t + 1, 1 - p, nth16(half, p, 1), True)
                    if tail and u == 7:
                        pe.wait_ge(oT_sb_s, t - 1)
                        mm(tail_ps[:, 1, :], oT_sb[:], w_back[:]).then_inc(f_ps_s, 1)
                    if prep and u == 8:
                        prep_products(t + 1)
                    if tail and u == 12:
                        pe.wait_ge(si_ready, t - 1)
                        nc.tensor.transpose(tail_ps[:, 3, :], si_cols[:], ident[:]).then_inc(score_ps_s, 1)
                    if pairs:
                        pe.wait_ge(h_ready, t * UNITS + u + 1)
                        for k in range(u * QPU, (u + 1) * QPU):
                            if not (early == 0 and k < YRING):
                                pe.wait_ge(q_done, t * QUARTS + k - YRING + 1)
                            for n in range(QUART):
                                last = mm(y_ps[k % YRING][:, n, :], h[:, u % HRING, (k % QPU) * QUART + n, :], w_pair[:])
                            last.then_inc(y_in_psum, 1)
                    chunk = (u + 1 - WEIGHTS_UNIT) // CHUNK_STEP - 1
                    chunk_due = (u + 1 - WEIGHTS_UNIT) % CHUNK_STEP == 0
                    if gather and chunk_due and chunk >= 0:
                        if chunk == 0:
                            pe.wait_ge(w_ready, t)
                            if early >= 2:
                                pe.wait_ge(o_stored, t - 1)
                        weighted_sums(1 - p, chunk)
                    if tail and chunk_due and chunk < 0:
                        weighted_sums(p, chunk + CHUNKS)

            run_slots(pe, slot)


_INS = ["x", "adj", "L0_gnn_W1", "L0_gnn_b1", "L0_gnn_W2", "L0_gnn_b2", "L0_gnn_gamma", "L0_gnn_beta",
        "L1_gnn_W_w", "L1_gnn_W_b", "L1_gnn_a_w", "L1_gnn_a_b"]


def kernel(**inputs):
    import numpy as _np
    import concourse.bacc as _bacc
    from concourse import mybir as _mybir
    from concourse.bass_utils import run_bass_kernel_spmd as _run

    nc = _bacc.Bacc("TRN2", target_bir_lowering=False, num_devices=1)
    arrays, args = {}, []
    for name in _INS:
        a = _np.ascontiguousarray(inputs[name])
        if a.ndim == 0:
            a = a.reshape(1, 1)
        arrays[f"in_{name}_dram"] = a
        args.append(nc.dram_tensor(f"in_{name}_dram", a.shape, _mybir.dt.from_np(a.dtype), kind="ExternalInput").ap())
    out = nc.dram_tensor("out_dram", inputs["x"].shape, _mybir.dt.float32, kind="ExternalOutput").ap()
    gnn_pair_kernel(nc, *args, out)
    r = _run(nc, [arrays], core_ids=[0])
    return r.results[0]["out_dram"]
```

```python
from contextlib import ExitStack
from math import sqrt

import concourse.bass as bass
from concourse import mybir


def gnn_pair_kernel(nc, x, adj, W1, b1, W2, b2, gamma, beta, Ww, Wb, aw, ab, out):
    F32 = mybir.dt.float32
    ALU = mybir.AluOpType
    ACT = mybir.ActivationFunctionType

    B, S, H = x.shape
    K = W2.shape[0]
    EPS = 1e-5
    UNIT = 8
    UNITS = S // UNIT
    QUART = 4
    QUARTS = S // QUART
    QPU = UNIT // QUART
    HRING = 4
    YRING = 4
    GROUPS, GROUP = 4, 32
    LAST = S - 1
    PEEL, LOOP_END = 4, B - 2

    CHUNK = 4
    CHUNKS = GROUP // CHUNK
    WEIGHTS_UNIT = 4
    POOL_WEIGHTS_UNIT = 8
    CHUNK_STEP = UNITS // CHUNKS
    EARLY_CHUNKS = (UNITS - WEIGHTS_UNIT) // CHUNK_STEP

    ctx = ExitStack()
    with ctx:
        def sb(name, shape):
            return ctx.enter_context(nc.sbuf_tensor(name, shape, F32))

        def ps(name, shape):
            return ctx.enter_context(nc.psum_tensor(name, shape, F32))

        def sem(name):
            return ctx.enter_context(nc.semaphore(name))

        w1a, w1b = sb("w1a", [H, K]), sb("w1b", [H, K])
        w2, w2T = sb("w2", [K, K]), sb("w2T", [K, K])
        b1c, b2col, gcol = sb("b1c", [K, 1]), sb("b2col", [K, 1]), sb("gcol", [K, 1])
        beta_rows = sb("beta_rows", [S, K])
        ww, wbc = sb("ww", [K, K]), sb("wbc", [K, 1])
        a1c, a2c, abc = sb("a1c", [K, 1]), sb("a2c", [K, 1]), sb("abc", [S, 1])
        ident, ones = sb("ident", [S, S]), sb("ones", [S, S])
        house, centre = sb("house", [K, K]), sb("centre", [K, K])
        basis, basis_half = sb("basis", [K, K]), sb("basis_half", [K, K])
        b2c, b2c_rep = sb("b2c", [K, 1]), sb("b2c_rep", [K, S])
        gdiag = sb("gdiag", [K, K])
        a1rep, a2rep, wbrep, a12 = sb("a1rep", [K, S]), sb("a2rep", [K, S]), sb("wbrep", [K, S]), sb("a12", [K, 1])
        w_pair = sb("w_pair", [K, K])
        w_back = sb("w_back", [K, K])
        v1row, v2row = sb("v1row", [S, K]), sb("v2row", [S, K])
        score_c = sb("score_c", [S, 1])
        bnorm = sb("bnorm", [S, 1])
        epsc = sb("epsc", [S, 1])

        x_in, adj_in = sb("x_in", [S, 2, H]), sb("adj_in", [S, 2, S])
        x_res, adj_res = sb("x_res", [S, 2, H]), sb("adj_res", [S, 2, S])
        adj_sum, x_beta = sb("adj_sum", [S, 1]), sb("x_beta", [S, H])
        sj, si, si_cols, s_terms = sb("sj", [S, 1]), sb("si", [S, 1]), sb("si_cols", [S, S]), sb("s_terms", [S, 2, K])
        xT = sb("xT", [H, S])
        adjT, adjS = sb("adjT", [S, 2, S]), sb("adjS", [S, 2, S])
        aT, bT = sb("aT", [K, 2, S]), sb("bT", [K, 2, S])
        h = sb("h", [K, HRING, UNIT, S])
        y = sb("y", [S, 2, S, K])
        squares = ctx.enter_context(nc.sbuf_tensor("squares", [S, YRING, QUART, K], mybir.dt.bfloat16))
        q = sb("q", [S, 2, S])
        v, sd = sb("v", [S, S]), sb("sd", [S, S])
        rstd = sb("rstd", [S, S])
        wz = sb("wz", [S, GROUPS, CHUNKS, GROUP])
        part = sb("part", [S, CHUNK])
        o_sb, oT_sb = sb("o_sb", [S, K]), sb("oT_sb", [K, S])
        x1p, x1e = sb("x1p", [S, K]), sb("x1e", [S, K + 1])
        st1, mv1, sd1, rs1 = sb("st1", [S, 6]), sb("mv1", [S, 2]), sb("sd1", [S, 1]), sb("rs1", [S, 1])
        ex, eT = sb("ex", [S, S]), sb("eT", [S, S])
        rz, x2p = sb("rz", [S, 1]), sb("x2p", [S, K])
        st2, mv2, sd2, rs2 = sb("st2", [S, 6]), sb("mv2", [S, 2]), sb("sd2", [S, 1]), sb("rs2", [S, 1])
        x_out = sb("x_out", [S, K])

        y_ps = [ps(f"y_ps{n}", [S, QUART, K]) for n in range(YRING)]
        agg_ps = ps("agg_ps", [S, 512])
        prep_ps = ps("prep_ps", [S, 4, 128])
        tail_ps = ps("tail_ps", [S, 4, 128])
        att_ps = ps("att_ps", [S, 512])

        s_w, s_w1 = sem("weights_loaded"), sem("first_layer_weights_loaded")
        s_const = sem("constants_built")
        s_setup_pe = sem("setup_products")
        s_setup_dve = sem("setup_vector_steps")
        s_ready = sem("setup_done")
        s_two, s_zero, s_part = sem("twos_preset"), sem("wz_zeroed"), sem("parts_marked")
        x_loaded, adj_loaded, xres_loaded, stored = (
            [sem(f"{n}_{p}") for p in range(2)] for n in ("x_loaded", "adj_loaded", "xres_loaded", "out_stored"))
        xT_ps_s, adjT_ps_s, adjT_sb_s = sem("xT_in_psum"), sem("adjT_in_psum"), sem("adjT_in_sbuf")
        ab_ps_s, ab_sb_s = sem("ab_in_psum"), sem("ab_in_sbuf")
        u_ready, h_ready = sem("preact_ready"), sem("h_ready")
        y_in_psum, y_stored, q_done = sem("y_in_psum"), sem("y_stored"), sem("q_done")
        v_ready, sd_ready, rstd_ready, w_ready, adjS_ready = sem("v_ready"), sem("sd_ready"), sem("rstd_ready"), sem("w_ready"), sem("adjS_ready")
        agg_done, o_part, o_stored, oT_ps_s, oT_sb_s, f_ps_s = sem("agg_done"), sem("o_part"), sem("o_stored"), sem("oT_in_psum"), sem("oT_in_sbuf"), sem("f_in_psum")
        x1p_ready, st1_ready, mv1_ready, sd1_ready, rs1_ready = sem("x1p_ready"), sem("st1_ready"), sem("mv1_ready"), sem("sd1_ready"), sem("rs1_ready")
        x1_ready, score_ps_s = sem("x1_ready"), sem("scores_in_psum")
        ex_ready, eT_ready, att_done = sem("exp_ready"), sem("eT_ready"), sem("attention_in_psum")
        rz_ready, x2p_ready, st2_ready, mv2_ready, sd2_ready, rs2_ready = sem("rz_ready"), sem("x2p_ready"), sem("st2_ready"), sem("mv2_ready"), sem("sd2_ready"), sem("rs2_ready")
        adj_sum_ready, x_beta_ready, sj_ready, si_sum_ready, si_ready = (
            sem(n) for n in ("adj_sum_ready", "x_beta_ready", "sj_ready", "si_sum_ready", "si_ready"))
        s_passed = sem("statistics_wait_passed")
        out_ready = sem("out_ready")

        def run_slots(engine, slot):
            for t in range(PEEL):
                slot(t, t // 2, t % 2, True, True, t >= 1, t >= 2, t >= 3, t)
            with engine.Fori(PEEL // 2, LOOP_END // 2) as pair:
                for p in range(2):
                    slot(pair * 2 + p, pair, p, True, True, True, True, True, PEEL)
            for t in range(LOOP_END, B + 3):
                slot(t, t // 2, t % 2, t < B, t + 1 < B, t <= B, t <= B + 1, True, PEEL)

        def nth16(half, p, off):
            return (half + (p + off) // 2 + 1) * 16

        block = ctx.enter_context(nc.Block())

        @block.sync
        def _(sp):
            for b in range(2):
                sp.dma_start(x_in[:, b, :], x[b]).then_inc(x_loaded[b], 16)
                sp.dma_start(adj_in[:, b, :], adj[b]).then_inc(adj_loaded[b], 16)
                if b == 0:
                    sp.dma_start(w1a[:], W1[0:H, :]).then_inc(s_w1, 16)
                    sp.dma_start(w1b[:], W1[H:2 * H, :]).then_inc(s_w1, 16)
                    sp.dma_start(b1c[:], b1.rearrange("(p o) -> p o", o=1)).then_inc(s_w1, 16)

            def slot(t, half, p, pairs, prep, gather, tail, finish, early):
                if pairs and not (isinstance(t, int) and t + 2 >= B):
                    sp.wait_ge(xT_ps_s, t + 1)
                    sp.dma_start(x_in[:, p, :], x[bass.ds(t + 2, 1)].rearrange("o s h -> (o s) h")).then_inc(x_loaded[p], 16)
                    sp.wait_ge(adjT_ps_s, t + 1)
                    sp.dma_start(adj_in[:, p, :], adj[bass.ds(t + 2, 1)].rearrange("o s h -> (o s) h")).then_inc(adj_loaded[p], 16)
                if gather:
                    if early >= 3:
                        sp.wait_ge(x1p_ready, t - 2)
                    sp.dma_start(x_res[:, 1 - p, :], x[bass.ds(t - 1, 1)].rearrange("o s h -> (o s) h")).then_inc(xres_loaded[1 - p], 16)
                    sp.dma_start(adj_res[:, 1 - p, :], adj[bass.ds(t - 1, 1)].rearrange("o s h -> (o s) h")).then_inc(xres_loaded[1 - p], 16)
                if finish:
                    sp.wait_ge(out_ready, t - 2)
                    sp.dma_start(out[bass.ds(t - 3, 1)].rearrange("o s h -> (o s) h"), x_out[:]).then_inc(stored[1 - p], 16)

            run_slots(sp, slot)
            for p in range(2):
                sp.wait_ge(stored[p], 16 * (B // 2))

        @block.gpsimd
        def _(pool):
            nc.gpsimd.memset(ident[:], 0.0).then_inc(s_const, 1)
            nc.gpsimd.memset(house[:], -1.0 / (K - sqrt(K))).then_inc(s_const, 1)
            nc.gpsimd.memset(ones[:], 1.0).then_inc(s_const, 1)
            pool.wait_ge(s_const, 3)
            nc.gpsimd.affine_select(out=ident[:], in_=ident[:], compare_op=ALU.not_equal, fill=1.0, base=0,
                                    pattern=[[-1, S]], channel_multiplier=1).then_inc(s_const, 1)
            nc.gpsimd.affine_select(out=house[:], in_=house[:], compare_op=ALU.not_equal, fill=1.0 / sqrt(K),
                                    base=-(K - 1), pattern=[[0, K]], channel_multiplier=1).then_inc(s_const, 1)
            nc.gpsimd.memset(epsc[:], EPS).then_inc(s_const, 1)

            def pair_weights(t, p, early):
                pool.wait_ge(rstd_ready, t)
                pool.wait_ge(adjT_sb_s, t)
                if early >= 2:
                    pool.wait_ge(agg_done, (t - 1) * CHUNKS)
                else:
                    pool.wait_ge(s_zero, 1)
                if early >= 3:
                    pool.wait_ge(eT_ready, t - 2)
                flat = wz[:]
                columns = bass.AP(flat.tensor, flat.offset,
                                  [list(flat.ap[0]), [CHUNKS * GROUP, GROUPS], [GROUP + CHUNK, CHUNKS], [1, CHUNK]])
                nc.gpsimd.tensor_tensor(columns, adjT[:, 1 - p, :].rearrange("j (g c s) -> j g c s", g=GROUPS, s=CHUNK),
                                        rstd[:].rearrange("j (c s g) -> j g c s", g=GROUPS, s=CHUNK), ALU.mult).then_inc(w_ready, 1)
                nc.gpsimd.tensor_copy(adjS[:, 1 - p, :], adjT[:, 1 - p, :]).then_inc(adjS_ready, 1)

            def slot(t, half, p, pairs, prep, gather, tail, finish, early):
                for u in range(UNITS):
                    if gather and u == POOL_WEIGHTS_UNIT:
                        pair_weights(t, p, early)
                    if not pairs:
                        continue
                    if early == 0 and u == HRING:
                        nc.gpsimd.memset(wz[:], 0.0).then_inc(s_zero, 1)
                    if u == 0:
                        pool.wait_ge(ab_sb_s, t + 1)
                    if not (early == 0 and u < HRING):
                        pool.wait_ge(y_in_psum, t * QUARTS + (u - HRING + 1) * QPU)
                    shape = [K, QPU, GROUPS, S]
                    a_now = aT[:, p, :].rearrange("k (g r) -> k r g", g=GROUPS)[:, u * QPU:(u + 1) * QPU, :]
                    nc.gpsimd.tensor_tensor(
                        h[:, u % HRING].rearrange("k (r g) s -> k r g s", g=GROUPS),
                        bT[:, p, :].unsqueeze(1).unsqueeze(1).broadcast_to(shape),
                        a_now.unsqueeze(3).broadcast_to(shape), ALU.add).then_inc(u_ready, 1)

            run_slots(pool, slot)

        @block.scalar
        def _(act):
            def copy(dst, src):
                return nc.scalar.activation(dst, src, ACT.Copy)

            def prep_copies(b, early):
                act.wait_ge(adjT_ps_s, b + 1)
                if early >= 1:
                    act.wait_ge(ab_ps_s, b)
                copy(xT[:], prep_ps[:, 0, :])
                if early >= 2:
                    act.wait_ge(w_ready, b - 1)
                    act.wait_ge(adjS_ready, b - 1)

            def relu(t, u):
                act.wait_ge(u_ready, t * UNITS + u + 1)
                nc.scalar.activation(h[:, u % HRING], h[:, u % HRING], ACT.Relu).then_inc(h_ready, 1)

            col = lambda a: a.rearrange("(p o) -> p o", o=1)
            act.dma_start(b2col[:], col(b2)).then_inc(s_w, 16)
            act.dma_start(w2[:], W2[:, :]).then_inc(s_w, 16)
            act.dma_start(gcol[:], col(gamma)).then_inc(s_w, 16)
            act.dma_start(ww[:], Ww[:, :]).then_inc(s_w, 16)
            act.dma_start(wbc[:], col(Wb)).then_inc(s_w, 16)
            act.dma_start(a1c[:], col(aw[0:K])).then_inc(s_w, 16)
            act.dma_start(a2c[:], col(aw[K:2 * K])).then_inc(s_w, 16)
            act.dma_start(abc[:], ab.broadcast_to([S, 1])).then_inc(s_w, 16)
            act.dma_start(beta_rows[:], beta.rearrange("(o k) -> o k", o=1).broadcast_to([S, K])).then_inc(s_w, 16)
            prep_copies(0, 0)
            copy(adjT[:, 0, :], prep_ps[:, 1, :]).then_inc(adjT_sb_s, 1)
            for u in range(2):
                relu(0, u)

            def slot(t, half, p, pairs, prep, gather, tail, finish, early):
                for u in range(UNITS):
                    if gather and u == 2:
                        act.wait_ge(v_ready, t)
                        if early >= 2:
                            act.wait_ge(rstd_ready, t - 1)
                        nc.scalar.activation(sd[:], v[:], ACT.Sqrt, bias=epsc[:, 0:1], scale=1.0 / K).then_inc(sd_ready, 1)
                    if finish and u == 6:
                        act.wait_ge(mv2_ready, t - 2)
                        if early >= 4:
                            act.wait_ge(rs2_ready, t - 3)
                        nc.scalar.activation(sd2[:], mv2[:, 1:2], ACT.Sqrt, bias=epsc[:, 0:1]).then_inc(sd2_ready, 1)
                    if tail and u == 7:
                        act.wait_ge(oT_ps_s, t - 1)
                        if early >= 3:
                            act.wait_ge(f_ps_s, t - 2)
                        copy(oT_sb[:], tail_ps[:, 0, :]).then_inc(oT_sb_s, 1)
                    if prep and u == 8:
                        prep_copies(t + 1, early + 1)
                        copy(adjT[:, 1 - p, :], prep_ps[:, 1, :]).then_inc(adjT_sb_s, 1)
                    if tail and u == 10:
                        act.wait_ge(mv1_ready, t - 1)
                        if early >= 3:
                            act.wait_ge(rs1_ready, t - 2)
                        nc.scalar.activation(sd1[:], mv1[:, 1:2], ACT.Sqrt, bias=epsc[:, 0:1]).then_inc(sd1_ready, 1)
                    if tail and u == 14:
                        act.wait_ge(score_ps_s, t - 1)
                        if early >= 3:
                            act.wait_ge(eT_ready, t - 2)
                        act.wait_ge(sj_ready, t - 1)
                        nc.scalar.activation(ex[:], tail_ps[:, 3, :], ACT.Exp, bias=sj[:, 0:1]).then_inc(ex_ready, 1)
                    if pairs:
                        ahead = u + 2
                        if ahead < UNITS:
                            relu(t, ahead)
                        elif prep:
                            relu(t + 1, ahead - UNITS)
                        for k in range(u * QPU, (u + 1) * QPU):
                            if k == 0 and early >= 2:
                                act.wait_ge(agg_done, (t - 2) * CHUNKS + EARLY_CHUNKS)
                            if k == EARLY_CHUNKS * CHUNK and early >= 2:
                                act.wait_ge(agg_done, (t - 1) * CHUNKS)
                            if k == 0 and early == 0:
                                act.wait_ge(s_two, 2)
                            act.wait_ge(y_in_psum, t * QUARTS + k + 1)
                            copy(y[:, p, k * QUART:(k + 1) * QUART, 0:LAST],
                                 y_ps[k % YRING][:, :, 0:LAST]).then_inc(y_stored, 1)

            run_slots(act, slot)

        @block.vector
        def _(dve):
            def project(b, p):
                dve.wait_ge(ab_ps_s, b + 1)
                nc.vector.tensor_copy(aT[:, p, :], prep_ps[:, 2, :])
                nc.vector.tensor_scalar(bT[:, p, :], prep_ps[:, 3, :], b1c[:, 0:1], None, ALU.add).then_inc(ab_sb_s, 1)

            for p in range(2):
                nc.vector.memset(y[:, p, :, LAST:S], 2.0).then_inc(s_two, 1)
            nc.vector.memset(x1e[:], 1.0).then_inc(s_setup_dve, 1)
            dve.wait_ge(s_const, 6)
            nc.vector.reduce_sum(part[:], ident[:].rearrange("p (c s) -> p s c", s=CHUNK), axis=mybir.AxisListType.X).then_inc(s_part, 1)
            nc.vector.tensor_scalar(centre[:], ident[:], -1.0 / K, None, ALU.add).then_inc(s_setup_dve, 1)
            nc.vector.tensor_tensor(basis[:], house[:], ident[:], ALU.add).then_inc(s_setup_dve, 1)
            dve.wait_ge(s_w, 16 * 9)
            nc.vector.tensor_scalar(gdiag[:], ident[:], gcol[:, 0:1], None, ALU.mult).then_inc(s_setup_dve, 1)
            nc.vector.tensor_scalar(a1rep[:], ones[:], a1c[:, 0:1], None, ALU.mult).then_inc(s_setup_dve, 1)
            nc.vector.tensor_scalar(a2rep[:], ones[:], a2c[:, 0:1], None, ALU.mult).then_inc(s_setup_dve, 1)
            nc.vector.tensor_scalar(wbrep[:], ones[:], wbc[:, 0:1], None, ALU.mult).then_inc(s_setup_dve, 1)
            nc.vector.tensor_tensor(a12[:], a1c[:], a2c[:], ALU.add).then_inc(s_setup_dve, 1)
            dve.wait_ge(s_setup_pe, 5)
            dve.wait_ge(s_setup_dve, 8)
            nc.vector.tensor_copy(b2c[:], att_ps[:, 0:1]).then_inc(s_setup_dve, 1)
            nc.vector.tensor_copy(basis[:, LAST:S], att_ps[:, 0:1]).then_inc(s_setup_dve, 1)
            dve.wait_ge(s_setup_dve, 10)
            nc.vector.tensor_scalar(b2c_rep[:], ones[:], b2c[:, 0:1], None, ALU.mult).then_inc(s_setup_dve, 1)
            nc.vector.tensor_copy(basis_half[:, 0:LAST], basis[:, 0:LAST]).then_inc(s_setup_dve, 1)
            nc.vector.tensor_scalar(basis_half[:, LAST:S], basis[:, LAST:S], 0.5, None, ALU.mult).then_inc(s_setup_dve, 1)
            nc.vector.tensor_copy(w2T[:], tail_ps[:, 0, :]).then_inc(s_setup_dve, 1)
            dve.wait_ge(s_w1, 16 * 3)
            project(0, 0)
            nc.vector.tensor_copy(v1row[:], tail_ps[:, 1, :]).then_inc(s_ready, 1)
            nc.vector.tensor_copy(v2row[:], tail_ps[:, 2, :]).then_inc(s_ready, 1)
            nc.vector.tensor_tensor(score_c[:], tail_ps[:, 3, 0:1], abc[:], ALU.add).then_inc(s_ready, 1)
            dve.wait_ge(s_setup_pe, 8)
            nc.vector.tensor_copy(bnorm[:], att_ps[:, 1:2]).then_inc(s_ready, 1)
            nc.vector.tensor_copy(w_pair[:], agg_ps[:, 0:K]).then_inc(s_ready, 1)
            nc.vector.tensor_copy(w_back[:], agg_ps[:, K:2 * K]).then_inc(s_ready, 1)
            dve.wait_ge(s_ready, 6)
            dve.wait_ge(s_part, 1)

            def slot(t, half, p, pairs, prep, gather, tail, finish, early):
                for u, e in ((u, e) for u in range(UNITS) for e in range(2 * QPU)):
                    if gather and (u, e) == (0, 0):
                        dve.wait_ge(q_done, t * QUARTS)
                        if early >= 2:
                            dve.wait_ge(sd_ready, t - 1)
                        nc.vector.tensor_scalar(v[:], q[:, 1 - p, :], bnorm[:, 0:1], 0.0, ALU.add, ALU.max).then_inc(v_ready, 1)
                    if finish and (u, e) == (4, 2):
                        dve.wait_ge(att_done, t - 2)
                        nc.vector.reciprocal(rz[:], att_ps[:, K:K + 1]).then_inc(rz_ready, 1)
                    if finish and (u, e) == (4, 3):
                        dve.wait_ge(rz_ready, t - 2)
                        nc.vector.scalar_tensor_tensor(out=x2p[:], in0=att_ps[:, 0:K], scalar=rz[:, 0:1], in1=x1e[:, 0:K],
                                                       op0=ALU.mult, op1=ALU.add).then_inc(x2p_ready, 1)
                    if finish and (u, e) == (5, 0):
                        dve.wait_ge(x2p_ready, t - 2)
                        nc.vector.bn_stats(st2[:], x2p[:]).then_inc(st2_ready, 1)
                    if finish and (u, e) == (5, 1):
                        dve.wait_ge(st2_ready, t - 2)
                        dve.sem_inc(s_passed, 1)
                        nc.vector.bn_aggr(mv2[:], st2[:]).then_inc(mv2_ready, 1)
                    if gather and (u, e) == (2, 0):
                        dve.wait_ge(sd_ready, t)
                        if early >= 2:
                            dve.wait_ge(w_ready, t - 1)
                        nc.vector.reciprocal(rstd[:], sd[:]).then_inc(rstd_ready, 1)
                    if finish and (u, e) == (7, 2):
                        dve.wait_ge(sd2_ready, t - 2)
                        nc.vector.reciprocal(rs2[:], sd2[:]).then_inc(rs2_ready, 1)
                    if finish and (u, e) == (8, 0):
                        dve.wait_ge(rs2_ready, t - 2)
                        if early >= 4:
                            dve.wait_ge(stored[p], nth16(half, p, -4))
                        nc.vector.tensor_scalar(x_out[:], x2p[:], mv2[:, 0:1], rs2[:, 0:1], ALU.subtract, ALU.mult).then_inc(out_ready, 1)
                    if tail and (u, e) == (3, 0):
                        dve.wait_ge(agg_done, (t - 1) * CHUNKS)
                        if early >= 3:
                            dve.wait_ge(oT_ps_s, t - 2)
                        nc.vector.tensor_scalar(o_sb[:], agg_ps[:, 0:K], part[:, 0:1], None, ALU.mult).then_inc(o_part, 1)
                    if tail and u == 3 and 1 <= e < CHUNK:
                        dve.wait_ge(o_part, (t - 2) * (CHUNK - 1) + e)
                        nc.vector.scalar_tensor_tensor(out=o_sb[:], in0=agg_ps[:, e * K:(e + 1) * K], scalar=part[:, e:e + 1],
                                                       in1=o_sb[:], op0=ALU.mult, op1=ALU.add).then_inc(
                                                           o_stored if e == CHUNK - 1 else o_part, 1)
                    if tail and (u, e) == (6, 0):
                        dve.wait_ge(xres_loaded[p], nth16(half, p, -2) * 2)
                        nc.vector.reduce_sum(adj_sum[:], adj_res[:, p, :], axis=mybir.AxisListType.X).then_inc(adj_sum_ready, 1)
                    if tail and (u, e) == (7, 0):
                        dve.wait_ge(adj_sum_ready, t - 1)
                        nc.vector.scalar_tensor_tensor(out=x_beta[:], in0=beta_rows[:], scalar=adj_sum[:, 0:1], in1=x_res[:, p, :],
                                                       op0=ALU.mult, op1=ALU.add).then_inc(x_beta_ready, 1)
                    if tail and (u, e) == (8, 1):
                        dve.wait_ge(x_beta_ready, t - 1)
                        dve.wait_ge(f_ps_s, t - 1)
                        nc.vector.tensor_tensor(x1p[:], tail_ps[:, 1, :], x_beta[:], ALU.add).then_inc(x1p_ready, 1)
                    if tail and (u, e) == (8, 2):
                        dve.wait_ge(x1p_ready, t - 1)
                        nc.vector.bn_stats(st1[:], x1p[:]).then_inc(st1_ready, 1)
                    if tail and (u, e) == (8, 3):
                        dve.wait_ge(st1_ready, t - 1)
                        dve.sem_inc(s_passed, 1)
                        nc.vector.bn_aggr(mv1[:], st1[:]).then_inc(mv1_ready, 1)
                    if prep and (u, e) == (10, 0):
                        if early >= 1:
                            dve.wait_ge(u_ready, t * UNITS)
                        project(t + 1, 1 - p)
                    if tail and (u, e) == (10, 2):
                        dve.wait_ge(sd1_ready, t - 1)
                        nc.vector.reciprocal(rs1[:], sd1[:]).then_inc(rs1_ready, 1)
                    if tail and (u, e) == (10, 3):
                        dve.wait_ge(rs1_ready, t - 1)
                        nc.vector.tensor_scalar(x1e[:, 0:K], x1p[:], mv1[:, 0:1], rs1[:, 0:1], ALU.subtract, ALU.mult).then_inc(x1_ready, 1)
                    if tail and (u, e) == (11, 0):
                        dve.wait_ge(x1_ready, t - 1)
                        nc.vector.tensor_tensor_reduce(out=s_terms[:, 1, :], in0=x1e[:, 0:K], in1=v1row[:], scale=1.0, scalar=0.0,
                                                       op0=ALU.mult, op1=ALU.add, accum_out=si[:, 0:1]).then_inc(si_sum_ready, 1)
                    if tail and (u, e) == (11, 1):
                        dve.wait_ge(si_sum_ready, t - 1)
                        if early >= 3:
                            dve.wait_ge(ex_ready, t - 2)
                        nc.vector.tensor_scalar(si_cols[:], ones[:], si[:, 0:1], None, ALU.mult).then_inc(si_ready, 1)
                    if tail and (u, e) == (12, 0):
                        if early >= 3:
                            dve.wait_ge(ex_ready, t - 2)
                        nc.vector.tensor_tensor_reduce(out=s_terms[:, 0, :], in0=x1e[:, 0:K], in1=v2row[:], scale=1.0, scalar=score_c[:, 0:1],
                                                       op0=ALU.mult, op1=ALU.add, accum_out=sj[:, 0:1]).then_inc(sj_ready, 1)
                    if tail and (u, e) == (14, 2):
                        dve.wait_ge(ex_ready, t - 1)
                        dve.wait_ge(adjS_ready, t - 1)
                        nc.vector.tensor_tensor(eT[:], ex[:], adjS[:, p, :], ALU.mult).then_inc(eT_ready, 1)
                    if pairs:
                        k = u * QPU + e // 2
                        if e % 2 == 0:
                            dve.wait_ge(y_stored, t * QUARTS + k + 1)
                        for n in range(e % 2 * 2, e % 2 * 2 + 2):
                            i = k * QUART + n
                            last = nc.vector.tensor_tensor_reduce(
                                out=squares[:, k % YRING, n, :], in0=y_ps[k % YRING][:, n, :], in1=y[:, p, i, :],
                                scale=1.0, scalar=0.0, op0=ALU.mult, op1=ALU.add, accum_out=q[:, p, i:i + 1])
                        if e % 2 == 1:
                            last.then_inc(q_done, 1)

            run_slots(dve, slot)

        @block.tensor
        def _(pe):
            def mm(dst, lhsT, rhs, start=True, stop=True):
                return nc.tensor.matmul(dst, lhsT, rhs, start=start, stop=stop)

            def prep_transposes(b, p, loads, later):
                pe.wait_ge(x_loaded[p], loads)
                if later:
                    pe.wait_ge(ab_sb_s, b)
                nc.tensor.transpose(prep_ps[:, 0, :], x_in[:, p, :], ident[:]).then_inc(xT_ps_s, 1)
                pe.wait_ge(adj_loaded[p], loads)
                nc.tensor.transpose(prep_ps[:, 1, :], adj_in[:, p, :], ident[:]).then_inc(adjT_ps_s, 1)

            def prep_products(b):
                pe.wait_ge(adjT_sb_s, b + 1)
                mm(prep_ps[:, 2, :], w1a[:], xT[:])
                mm(prep_ps[:, 3, :], w1b[:], xT[:]).then_inc(ab_ps_s, 1)

            pe.wait_ge(s_const, 6)
            prep_transposes(0, 0, 16, False)
            pe.wait_ge(s_w, 16 * 9)
            pe.wait_ge(s_setup_dve, 8)
            mm(att_ps[:, 0:1], centre[:], b2col[:]).then_inc(s_setup_pe, 1)
            nc.tensor.transpose(tail_ps[:, 0, :], w2[:], ident[:]).then_inc(s_setup_pe, 1)
            mm(tail_ps[:, 1, :], a1rep[:], ww[:]).then_inc(s_setup_pe, 1)
            mm(tail_ps[:, 2, :], a2rep[:], ww[:]).then_inc(s_setup_pe, 1)
            mm(tail_ps[:, 3, 0:1], wbrep[:], a12[:]).then_inc(s_setup_pe, 1)
            pe.wait_ge(s_w1, 16 * 3)
            prep_products(0)
            pe.wait_ge(s_setup_dve, 14)
            mm(att_ps[:, 1:2], b2c_rep[:], b2c[:]).then_inc(s_setup_pe, 1)
            mm(agg_ps[:, 0:K], w2T[:], basis[:]).then_inc(s_setup_pe, 1)
            mm(agg_ps[:, K:2 * K], basis_half[:], gdiag[:]).then_inc(s_setup_pe, 1)

            pe.wait_ge(s_ready, 6)

            def weighted_sums(b_parity, chunk):
                y_chunk = y[:, b_parity, chunk * CHUNK * GROUPS:(chunk + 1) * CHUNK * GROUPS, :].rearrange(
                    "j (r g) m -> j r g m", g=GROUPS)
                for g in range(GROUPS):
                    last = nc.tensor.matmul(agg_ps[g * GROUP:(g + 1) * GROUP, :], wz[:, g, chunk, :], y_chunk[:, :, g, :],
                                            start=(chunk == 0), stop=(chunk == CHUNKS - 1), tile_position=(0, g * GROUP))
                last.then_inc(agg_done, 1)

            def slot(t, half, p, pairs, prep, gather, tail, finish, early):
                for u in range(UNITS):
                    if finish and u == 0:
                        pe.wait_ge(eT_ready, t - 2)
                        mm(att_ps[:, 0:K + 1], eT[:], x1e[:]).then_inc(att_done, 1)
                    if tail and u == 6:
                        pe.wait_ge(o_stored, t - 1)
                        nc.tensor.transpose(tail_ps[:, 0, :], o_sb[:], ident[:]).then_inc(oT_ps_s, 1)
                    if prep and u == 6:
                        prep_transposes(t + 1, 1 - p, nth16(half, p, 1), True)
                    if tail and u == 8:
                        pe.wait_ge(oT_sb_s, t - 1)
                        mm(tail_ps[:, 1, :], oT_sb[:], w_back[:]).then_inc(f_ps_s, 1)
                    if prep and u == 9:
                        prep_products(t + 1)
                    if tail and u == 13:
                        pe.wait_ge(si_ready, t - 1)
                        nc.tensor.transpose(tail_ps[:, 3, :], si_cols[:], ident[:]).then_inc(score_ps_s, 1)
                    if pairs:
                        pe.wait_ge(h_ready, t * UNITS + u + 1)
                        for k in range(u * QPU, (u + 1) * QPU):
                            if not (early == 0 and k < YRING):
                                pe.wait_ge(q_done, t * QUARTS + k - YRING + 1)
                            for n in range(QUART):
                                last = mm(y_ps[k % YRING][:, n, :], h[:, u % HRING, (k % QPU) * QUART + n, :], w_pair[:])
                            last.then_inc(y_in_psum, 1)
                    chunk = (u + 1 - WEIGHTS_UNIT) // CHUNK_STEP - 1
                    chunk_due = (u + 1 - WEIGHTS_UNIT) % CHUNK_STEP == 0
                    if gather and chunk_due and chunk >= 0:
                        if chunk == 0:
                            pe.wait_ge(w_ready, t)
                            if early >= 2:
                                pe.wait_ge(o_stored, t - 1)
                        weighted_sums(1 - p, chunk)
                    if tail and chunk_due and chunk < 0:
                        weighted_sums(p, chunk + CHUNKS)

            run_slots(pe, slot)


_INS = ["x", "adj", "L0_gnn_W1", "L0_gnn_b1", "L0_gnn_W2", "L0_gnn_b2", "L0_gnn_gamma", "L0_gnn_beta",
        "L1_gnn_W_w", "L1_gnn_W_b", "L1_gnn_a_w", "L1_gnn_a_b"]


def kernel(**inputs):
    import numpy as _np
    import concourse.bacc as _bacc
    from concourse import mybir as _mybir
    from concourse.bass_utils import run_bass_kernel_spmd as _run

    nc = _bacc.Bacc("TRN2", target_bir_lowering=False, num_devices=1)
    arrays, args = {}, []
    for name in _INS:
        a = _np.ascontiguousarray(inputs[name])
        if a.ndim == 0:
            a = a.reshape(1, 1)
        arrays[f"in_{name}_dram"] = a
        args.append(nc.dram_tensor(f"in_{name}_dram", a.shape, _mybir.dt.from_np(a.dtype), kind="ExternalInput").ap())
    out = nc.dram_tensor("out_dram", inputs["x"].shape, _mybir.dt.float32, kind="ExternalOutput").ap()
    gnn_pair_kernel(nc, *args, out)
    r = _run(nc, [arrays], core_ids=[0])
    return r.results[0]["out_dram"]
```
